# Optimizing a Trainium2 kernel written in Bass

```python
import numpy as np
import jax
import jax.numpy as jnp

def _softmax(x, axis=-1):
    return jax.nn.softmax(x, axis=axis)

def _gelu(x):
    return jax.nn.gelu(x, approximate=True)

def _silu(x):
    return jax.nn.silu(x)

def _sigmoid(x):
    return jax.nn.sigmoid(x)

def _layernorm(x, axis=-1, eps=1e-05):
    m = jnp.mean(x, axis=axis, keepdims=True)
    v = jnp.var(x, axis=axis, keepdims=True)
    return (x - m) / jnp.sqrt(v + eps)

def _scatter_add(tgt, idx, src, axis=0):
    return tgt.at[idx].add(src)

def _segment_sum(src, seg, n):
    return jax.ops.segment_sum(src, seg, n)
kernel_name = 'mk_decoder_preln_d1_seqx_r8_2b5d64'

def setup_inputs(seed: int=0):
    np.random.seed(seed)
    _w = jnp.asarray

    def _rec_inputs():
        import jax
        import jax.numpy as jnp
        _rk = jax.random.key(seed)
        x = -0.0003929 + 0.9999 * jax.random.normal(jax.random.fold_in(_rk, 1), (16, 128, 128), jnp.float32)
        _lenS = 128 - jax.random.randint(jax.random.fold_in(_rk, 7), (16,), 0, max(1, 128 // 4) + 1, jnp.int32)
        _lenS2 = 77 - jax.random.randint(jax.random.fold_in(_rk, 8), (16,), 0, max(1, 77 // 4) + 1, jnp.int32)
        _ctx_768P = jax.random.normal(jax.random.fold_in(_rk, 11), (16, 16, 96), jnp.float32)
        _ctx_768c = jax.random.dirichlet(jax.random.fold_in(_rk, 511), 0.3 * jnp.ones((16,), jnp.float32), (16, 77))
        _ctx_768t = jnp.einsum('bsk,bkd->bsd', _ctx_768c, _ctx_768P)
        _ctx_768t = _ctx_768t * jax.lax.rsqrt(jnp.mean(jnp.square(_ctx_768t)) + 1e-12) * 0.953939
        ctx_768 = 0.00095986 + 0.999812 * (_ctx_768t + 0.3 * jax.random.normal(jax.random.fold_in(_rk, 611), (16, 77, 96), jnp.float32))
        _validS = jnp.arange(128)[None, :] < _lenS[:, None]
        _validS2 = jnp.arange(77)[None, :] < _lenS2[:, None]
        _causal = jnp.tril(jnp.ones((128, 128), dtype=bool))
        mask_BxS2_bf1 = jnp.ones((16, 77), dtype=bool)
        return (x, ctx_768, mask_BxS2_bf1)
    x, ctx_768, mask_BxS2_bf1 = _rec_inputs()

    def _L0_attn_setup():
        import jax, jax.numpy as jnp
        import numpy as np

        def _wkv_scan(key, value, time_decay, time_first):
            w = -jnp.exp(time_decay)
            B, T, C = key.shape

            def step(carry, kv):
                num, den, mx = carry
                k, v = kv
                mo = jnp.maximum(mx, k + time_first)
                e1 = jnp.exp(mx - mo)
                e2 = jnp.exp(k + time_first - mo)
                out = (e1 * num + e2 * v) / (e1 * den + e2)
                ms = jnp.maximum(mx + w, k)
                e1s = jnp.exp(mx + w - ms)
                e2s = jnp.exp(k - ms)
                return ((e1s * num + e2s * v, e1s * den + e2s, ms), out)
            init = (jnp.zeros((B, C), key.dtype), jnp.zeros((B, C), key.dtype), jnp.full((B, C), -1e+38, key.dtype))
            kT = jnp.swapaxes(key, 0, 1)
            vT = jnp.swapaxes(value, 0, 1)
            _, outs = jax.lax.scan(step, init, (kT, vT))
            return jnp.swapaxes(outs, 0, 1)
        key = jax.random.key(seed)
        ks = jax.random.split(key, 10)
        B, T, C = (8, 256, 128)
        s = 1.0 / np.sqrt(C)
        return {'x': jax.random.normal(ks[0], (B, T, C), jnp.float32), 'wk': jax.random.normal(ks[1], (C, C), jnp.float32) * s, 'wv': jax.random.normal(ks[2], (C, C), jnp.float32) * s, 'wr': jax.random.normal(ks[3], (C, C), jnp.float32) * s, 'wo': jax.random.normal(ks[4], (C, C), jnp.float32) * s, 'time_decay': jax.random.normal(ks[5], (C,), jnp.float32) * 0.5, 'time_first': jax.random.normal(ks[6], (C,), jnp.float32) * 0.5, 'mix_k': jax.random.uniform(ks[7], (1, 1, C), jnp.float32), 'mix_v': jax.random.uniform(ks[8], (1, 1, C), jnp.float32), 'mix_r': jax.random.uniform(ks[9], (1, 1, C), jnp.float32)}
    _L0_attn_all = _L0_attn_setup()
    _L0_attn_in = {k: v for k, v in _L0_attn_all.items() if k in ('wk', 'wv', 'wr', 'wo', 'time_decay', 'time_first', 'mix_k', 'mix_v', 'mix_r')}
    del _L0_attn_all

    def _L0_xattn_setup():
        import jax, jax.numpy as jnp
        import numpy as np
        DIM = 128
        CTX_DIM = 96
        HEADS = 16
        key = jax.random.key(seed)
        ks = jax.random.split(key, 7)
        B, N, M = (4, 512, 32)
        x = jax.random.normal(ks[0], (B, N, DIM), dtype=jnp.float32)
        context = jax.random.normal(ks[1], (B, M, CTX_DIM), dtype=jnp.float32)
        context_mask = jnp.ones((B, M), dtype=bool)
        s_d = 1.0 / np.sqrt(DIM)
        s_c = 1.0 / np.sqrt(CTX_DIM)
        Wq = jax.random.normal(ks[2], (DIM, DIM), dtype=jnp.float32) * s_d
        Wk = jax.random.normal(ks[3], (CTX_DIM, DIM), dtype=jnp.float32) * s_c
        Wv = jax.random.normal(ks[4], (CTX_DIM, DIM), dtype=jnp.float32) * s_c
        Wo = jax.random.normal(ks[5], (DIM, DIM), dtype=jnp.float32) * s_d
        return {'x': x, 'context': context, 'context_mask': context_mask, 'Wq': Wq, 'Wk': Wk, 'Wv': Wv, 'Wo': Wo}
    _L0_xattn_all = _L0_xattn_setup()
    _L0_xattn_in = {k: v for k, v in _L0_xattn_all.items() if k in ('Wq', 'Wk', 'Wv', 'Wo')}
    del _L0_xattn_all

    def _L0_ffn_setup():
        import jax, jax.numpy as jnp
        import numpy as np
        ALPHA = 1.5
        TEMP = 1.0
        N_ITER = 25
        THRESH = 1e-09

        def entmax_bisect(X, alpha=ALPHA, n_iter=N_ITER):
            d = X.shape[-1]
            inv_am1 = 1.0 / (alpha - 1.0)
            Xs = X * (alpha - 1.0)
            max_val = jnp.max(Xs, axis=-1, keepdims=True)
            tau_lo = max_val - 1.0
            tau_hi = max_val - (1.0 / d) ** (alpha - 1.0)
            f_lo = jnp.sum(jnp.maximum(Xs - tau_lo, 0.0) ** inv_am1, axis=-1, keepdims=True) - 1.0

            def body(i, carry):
                tau_lo, dm, _ = carry
                dm = dm * 0.5
                tau_m = tau_lo + dm
                f_m = jnp.sum(jnp.maximum(Xs - tau_m, 0.0) ** inv_am1, axis=-1, keepdims=True) - 1.0
                tau_lo = jnp.where(f_m * f_lo >= 0.0, tau_m, tau_lo)
                return (tau_lo, dm, tau_m)
            dm0 = tau_hi - tau_lo
            _, _, tau_m = jax.lax.fori_loop(0, n_iter, body, (tau_lo, dm0, tau_lo))
            p = jnp.maximum(Xs - tau_m, 0.0) ** inv_am1
            return p / jnp.sum(p, axis=-1, keepdims=True)
        key = jax.random.key(seed)
        ks = jax.random.split(key, 8)
        B, S, D, E = (2, 128, 128, 8)
        F = 4 * D
        return {'x': jax.random.normal(ks[0], (B, S, D), jnp.float32), 'Wr': jax.random.normal(ks[1], (D, E), jnp.float32) * 0.02, 'br': jnp.zeros((E,), jnp.float32), 'W1': jax.random.normal(ks[2], (E, D, F), jnp.float32) * 0.02, 'b1': jnp.zeros((E, F), jnp.float32), 'W2': jax.random.normal(ks[3], (E, F, D), jnp.float32) * 0.02, 'b2': jnp.zeros((E, D), jnp.float32)}
    _L0_ffn_all = _L0_ffn_setup()
    _L0_ffn_in = {k: v for k, v in _L0_ffn_all.items() if k in ('Wr', 'br', 'W1', 'b1', 'W2', 'b2')}
    del _L0_ffn_all
    return {'x': x, 'ctx_768': ctx_768, 'mask_BxS2_bf1': mask_BxS2_bf1, 'L0_attn_wk': _L0_attn_in['wk'], 'L0_attn_wv': _L0_attn_in['wv'], 'L0_attn_wr': _L0_attn_in['wr'], 'L0_attn_wo': _L0_attn_in['wo'], 'L0_attn_time_decay': _L0_attn_in['time_decay'], 'L0_attn_time_first': _L0_attn_in['time_first'], 'L0_attn_mix_k': _L0_attn_in['mix_k'], 'L0_attn_mix_v': _L0_attn_in['mix_v'], 'L0_attn_mix_r': _L0_attn_in['mix_r'], 'L0_xattn_Wq': _L0_xattn_in['Wq'], 'L0_xattn_Wk': _L0_xattn_in['Wk'], 'L0_xattn_Wv': _L0_xattn_in['Wv'], 'L0_xattn_Wo': _L0_xattn_in['Wo'], 'L0_ffn_Wr': _L0_ffn_in['Wr'], 'L0_ffn_br': _L0_ffn_in['br'], 'L0_ffn_W1': _L0_ffn_in['W1'], 'L0_ffn_b1': _L0_ffn_in['b1'], 'L0_ffn_W2': _L0_ffn_in['W2'], 'L0_ffn_b2': _L0_ffn_in['b2']}

def reference(x, ctx_768, mask_BxS2_bf1, L0_attn_wk, L0_attn_wv, L0_attn_wr, L0_attn_wo, L0_attn_time_decay, L0_attn_time_first, L0_attn_mix_k, L0_attn_mix_v, L0_attn_mix_r, L0_xattn_Wq, L0_xattn_Wk, L0_xattn_Wv, L0_xattn_Wo, L0_ffn_Wr, L0_ffn_br, L0_ffn_W1, L0_ffn_b1, L0_ffn_W2, L0_ffn_b2):
    import jax
    import jax.numpy as jnp

    def _L0_attn_ref(x, wk, wv, wr, wo, time_decay, time_first, mix_k, mix_v, mix_r):
        import jax, jax.numpy as jnp
        import numpy as np

        def _wkv_scan(key, value, time_decay, time_first):
            w = -jnp.exp(time_decay)
            B, T, C = key.shape

            def step(carry, kv):
                num, den, mx = carry
                k, v = kv
                mo = jnp.maximum(mx, k + time_first)
                e1 = jnp.exp(mx - mo)
                e2 = jnp.exp(k + time_first - mo)
                out = (e1 * num + e2 * v) / (e1 * den + e2)
                ms = jnp.maximum(mx + w, k)
                e1s = jnp.exp(mx + w - ms)
                e2s = jnp.exp(k - ms)
                return ((e1s * num + e2s * v, e1s * den + e2s, ms), out)
            init = (jnp.zeros((B, C), key.dtype), jnp.zeros((B, C), key.dtype), jnp.full((B, C), -1e+38, key.dtype))
            kT = jnp.swapaxes(key, 0, 1)
            vT = jnp.swapaxes(value, 0, 1)
            _, outs = jax.lax.scan(step, init, (kT, vT))
            return jnp.swapaxes(outs, 0, 1)
        prev_x = jnp.pad(x, ((0, 0), (1, 0), (0, 0)))[:, :-1, :]
        k_in = x * mix_k + prev_x * (1.0 - mix_k)
        v_in = x * mix_v + prev_x * (1.0 - mix_v)
        r_in = x * mix_r + prev_x * (1.0 - mix_r)
        key = jnp.einsum('btc,dc->btd', k_in, wk)
        value = jnp.einsum('btc,dc->btd', v_in, wv)
        receptance = jax.nn.sigmoid(jnp.einsum('btc,dc->btd', r_in, wr))
        wkv = _wkv_scan(key, value, time_decay, time_first)
        rwkv = receptance * wkv
        return jnp.einsum('btc,dc->btd', rwkv, wo)

    def _L0_xattn_ref(x, context, context_mask, Wq, Wk, Wv, Wo):
        import jax, jax.numpy as jnp
        import numpy as np
        DIM = 128
        CTX_DIM = 96
        HEADS = 16
        B, N, _ = x.shape
        M = context.shape[1]
        hd = DIM // HEADS
        scale = hd ** (-0.5)
        q = (x @ Wq).reshape(B, N, HEADS, hd).transpose(0, 2, 1, 3)
        k = (context @ Wk).reshape(B, M, HEADS, hd).transpose(0, 2, 1, 3)
        v = (context @ Wv).reshape(B, M, HEADS, hd).transpose(0, 2, 1, 3)
        scores = jnp.einsum('bhid,bhjd->bhij', q, k) * scale
        max_neg = -jnp.finfo(scores.dtype).max
        scores = jnp.where(context_mask[:, None, None, :], scores, max_neg)
        attn = jax.nn.softmax(scores, axis=-1)
        out = jnp.einsum('bhij,bhjd->bhid', attn, v)
        out = out.transpose(0, 2, 1, 3).reshape(B, N, DIM)
        return out @ Wo

    def _L0_ffn_ref(x, Wr, br, W1, b1, W2, b2):
        import jax, jax.numpy as jnp
        import numpy as np
        ALPHA = 1.5
        TEMP = 1.0
        N_ITER = 25
        THRESH = 1e-09

        def entmax_bisect(X, alpha=ALPHA, n_iter=N_ITER):
            d = X.shape[-1]
            inv_am1 = 1.0 / (alpha - 1.0)
            Xs = X * (alpha - 1.0)
            max_val = jnp.max(Xs, axis=-1, keepdims=True)
            tau_lo = max_val - 1.0
            tau_hi = max_val - (1.0 / d) ** (alpha - 1.0)
            f_lo = jnp.sum(jnp.maximum(Xs - tau_lo, 0.0) ** inv_am1, axis=-1, keepdims=True) - 1.0

            def body(i, carry):
                tau_lo, dm, _ = carry
                dm = dm * 0.5
                tau_m = tau_lo + dm
                f_m = jnp.sum(jnp.maximum(Xs - tau_m, 0.0) ** inv_am1, axis=-1, keepdims=True) - 1.0
                tau_lo = jnp.where(f_m * f_lo >= 0.0, tau_m, tau_lo)
                return (tau_lo, dm, tau_m)
            dm0 = tau_hi - tau_lo
            _, _, tau_m = jax.lax.fori_loop(0, n_iter, body, (tau_lo, dm0, tau_lo))
            p = jnp.maximum(Xs - tau_m, 0.0) ** inv_am1
            return p / jnp.sum(p, axis=-1, keepdims=True)
        B, S, D = x.shape
        xt = x.reshape(B * S, D)
        logits = (xt @ Wr + br) / TEMP
        gates = entmax_bisect(logits)
        gates = jnp.where(gates > THRESH, gates, 0.0)
        h = jax.nn.relu(jnp.einsum('td,edf->etf', xt, W1) + b1[:, None, :])
        y = jnp.einsum('etf,efd->etd', h, W2) + b2[:, None, :]
        out = jnp.einsum('etd,te->td', y, gates)
        return out.reshape(B, S, D)
    x = x + _L0_attn_ref(_layernorm(x, axis=-1), L0_attn_wk, L0_attn_wv, L0_attn_wr, L0_attn_wo, L0_attn_time_decay, L0_attn_time_first, L0_attn_mix_k, L0_attn_mix_v, L0_attn_mix_r)
    x = x + _L0_xattn_ref(_layernorm(x, axis=-1), ctx_768, mask_BxS2_bf1, L0_xattn_Wq, L0_xattn_Wk, L0_xattn_Wv, L0_xattn_Wo)
    x = x + _L0_ffn_ref(_layernorm(x, axis=-1), L0_ffn_Wr, L0_ffn_br, L0_ffn_W1, L0_ffn_b1, L0_ffn_W2, L0_ffn_b2)
    return x

_drawn_inputs = setup_inputs


def setup_inputs(seed=0):
    import zlib

    import numpy as np

    out = dict(_drawn_inputs(seed))
    spreads = {'L0_ffn_br': (0.0, 0.51), 'L0_ffn_b1': (0.0, 0.757), 'L0_ffn_b2': (0.0, 0.1)}
    factors = {}
    for name, (base, spread) in spreads.items():
        noise = np.random.default_rng([zlib.crc32(name.encode()), seed]).standard_normal(out[name].shape)
        drawn = base * np.exp(spread * noise) if base else spread * noise
        out[name] = jnp.asarray(drawn.astype(out[name].dtype))
    for name, factor in factors.items():
        out[name] = (out[name] * factor).astype(out[name].dtype)
    return out
```

```python
from contextlib import ExitStack

import concourse.bass as bass
from concourse import mybir

F32 = mybir.dt.float32
F32R = mybir.dt.float32r
BF16 = mybir.dt.bfloat16
U8 = mybir.dt.uint8
ALU = mybir.AluOpType
ACT = mybir.ActivationFunctionType
AX_X = mybir.AxisListType.X

P = 128
B, T, C = 16, 128, 128
GB = 4
G = B // GB
N = GB * T
TP = T + 1
NPAD = GB * TP
M, CTX = 77, 96
H, HD = 16, 8
QH = 4
NQ = H // QH
SQ = QH * M
KT = -(-SQ // P)
SP = KT * P
E, F = 8, 512
FT = F // P
NS = E * FT
UNITS = GB * NQ
NEWTON = 7
EPS = 1e-5
THRESH = 1e-9
NEG = -1e38
MASKED = 3.3895313892515355e38

ATT_START = 12
FFN_START = ATT_START + 22
SLOTS = 16

PACK = {}
_at = 0
for _name, _n in (("ident", P), ("qmask", QH), ("vmask", KT * H), ("cols", 5), ("wkT", C), ("wvT", C),
                  ("wrT", C), ("woT", C), ("Wq", C), ("Wo", C), ("Wr", E), ("b1", NS), ("b2", E)):
    PACK[_name] = (_at, _at + _n)
    _at += _n
PACKED = _at


def mixing_steps(g, r):
    return {
        0: [("stats", 0, g, None)],
        1: [("norm", 0, g, None), ("turn", 0, g, None)],
        2: [("key", g), ("value", g)],
        3: [("receptance", g), ("decay", g)],
        5: [("scans", g)],
        6: [("mix", g)],
        7: [("rwkv", g)],
        8: [("mixed", g)],
        9: [("stats", 1, g, None)],
        10: [("norm", 1, g, None), ("turn", 1, g, None)],
        11: [("query", g)],
    }.get(r, [])


def attention_steps(g, r):
    out = []
    if 3 <= r < UNITS + 3:
        out.append(("probs_v", g, r - 3))
    if r % NQ == 0 and r < UNITS:
        out.append(("context", g, r // NQ))
    if 1 <= r < UNITS + 1:
        out.append(("scores", g, r - 1))
    if 2 <= r < UNITS + 2:
        out.append(("turn_probs", g, r - 2))
    b, at = (r - 6) // NQ, (r - 6) % NQ
    if r >= 6 and b < GB:
        out += {0: [("turn_heads", g, b)], 1: [("attended", g, b), ("stats", 2, g, b)],
                2: [("norm", 2, g, b), ("turn", 2, g, b)]}.get(at, [])
    if r == 6 + NQ * (GB - 1) + 3:
        out.append(("router", g))
    return out


def expert_steps(g, r, half):
    s = 2 * r + half
    out = []
    if s < NS:
        out.append(("hidden", g, s))
    if 1 <= s <= NS:
        out.append(("down", g, s - 1))
    if s >= FT + 1 and s % FT == 1 and s // FT <= E:
        out.append(("gated", g, s // FT - 1))
    if s == NS + 1:
        out.append(("store", g))
    return out


def plan():
    steps = []
    for slot in range(SLOTS * (G - 1) + FFN_START + NS // 2 + 1):
        for half in range(2):
            for g in range(G):
                r = slot - SLOTS * g
                if r - FFN_START >= 0:
                    steps += expert_steps(g, r - FFN_START, half)
            for g in range(G):
                r = slot - SLOTS * g
                if half and r >= 0:
                    steps += mixing_steps(g, r)
                if not half and r >= ATT_START:
                    steps += attention_steps(g, r - ATT_START)
    return steps


def build(nc, x, ctxT, mask, pack, wkv96, br, w1, w2, out):
    steps = plan()
    nth = {}
    seen = {}
    for st in steps:
        seen[st[0]] = seen.get(st[0], 0) + 1
        nth[st] = seen[st[0]]
    SHARED = ("turn", "key", "value", "receptance", "mixed", "query", "context", "probs_v",
              "turn_heads", "attended", "router", "gated")
    shared = {st: i for i, st in enumerate(s for s in steps if s[0] in SHARED)}

    with ExitStack() as ctx:
        def sb(name, shape, dt=F32):
            return ctx.enter_context(nc.sbuf_tensor(name, shape, dt))

        def ps(name):
            return ctx.enter_context(nc.psum_tensor(name, [P, 512], F32))

        def sem(name):
            return ctx.enter_context(nc.semaphore(name))

        resid = sb("resid", [P, B, C])
        pk = sb("pk", [P, PACKED])
        w96 = sb("w96", [CTX, 2 * C])
        ctx_sb = sb("ctx_sb", [CTX, B, M])
        br_sb = sb("br_sb", [1, E])
        w1_raw = sb("w1_raw", [P, 2, F])
        w1_hi = sb("w1_hi", [P, E * F], F32R)
        w1_lo = sb("w1_lo", [P, E * F], F32R)
        w2_sb = sb("w2_sb", [P, NS * C])
        mask_u8 = sb("mask_u8", [P, B * M], U8)
        mask_bias = sb("mask_bias", [P, B, M], BF16)
        ones_b = sb("ones_b", [P, P], BF16)
        ones_f = sb("ones_f", [1, P])
        half_neg = sb("half_neg", [P, GB])
        mix_c = sb("mix_c", [P, 3])
        w_now = sb("w_now", [P, 3, C])
        w_before = sb("w_before", [P, 3, C])
        decay_w = sb("decay_w", [P, 1])
        decay_row = sb("decay_row", [P, NPAD])
        bn = sb("bn", [P, B, 6])
        mv = sb("mv", [P, 3, B, 2])
        var_e = sb("var_e", [P, 3, B])
        rstd = sb("rstd", [P, 3, B])
        xn = sb("xn", [P, B, C])
        xT1 = sb("xT1", [P, 2, NPAD])
        xT2 = sb("xT2", [P, N])
        xT3 = sb("xT3", [P, N])
        x_hi = sb("x_hi", [P, 2, N], F32R)
        x_lo = sb("x_lo", [P, 2, N], F32R)
        k_sb = sb("k_sb", [P, NPAD])
        v_sb = sb("v_sb", [P, NPAD])
        er = sb("er", [P, N])
        mx = sb("mx", [P, NPAD])
        ex = sb("ex", [P, 4, NPAD])
        ev = sb("ev", [P, NPAD])
        num = sb("num", [P, NPAD])
        den = sb("den", [P, NPAD])
        ta = sb("ta", [P, N])
        tb = sb("tb", [P, N])
        tc = sb("tc", [P, N])
        rwkv = sb("rwkv", [P, N])
        qT = sb("qT", [P, 2, N])
        ctx4 = sb("ctx4", [CTX, 2, SP])
        kbd = sb("kbd", [P, 2, SQ])
        vbd = sb("vbd", [P, 2, KT * H * (HD + 1)])
        smax = sb("smax", [P, 2, QH])
        prob = sb("prob", [P, 3, SP])
        probT = sb("probT", [P, 2, SP])
        rsum = sb("rsum", [P, 2, QH])
        heads = sb("heads", [P, 2, C])
        headsT = sb("headsT", [P, 2, C])
        xs = sb("xs", [P, GB, E])
        t8a = sb("t8a", [P, GB, E])
        t8b = sb("t8b", [P, GB, E])
        top = sb("top", [P, GB])
        tau = sb("tau", [P, GB])
        s1 = sb("s1", [P, GB])
        s2 = sb("s2", [P, GB])
        gates = sb("gates", [P, 2, GB, E])
        hid = sb("hid", [P, 3, N])
        yT = sb("yT", [P, 2, N])

        bank_z = [ps("bank_z0"), ps("bank_z1")]
        bank_y = ps("bank_y")
        bank_s = [ps("bank_s0"), ps("bank_s1")]
        bank_p = ps("bank_p")
        bank_m = [ps("bank_m0"), ps("bank_m1")]

        x_in = [sem(f"x_in{g}") for g in range(G)]
        pack_in, ctx_in, small_in = sem("pack_in"), sem("ctx_in"), sem("small_in")
        w1_in, w2_in = [sem(f"w1_in{e}") for e in range(E)], sem("w2_in")
        w1_split = sem("w1_split")
        pool_step = sem("pool_step")
        pool_const, dve_const, act_const = sem("pool_const"), sem("dve_const"), sem("act_const")
        dve_step = sem("dve_step")
        stats_ready, rstd_ready, normed = sem("stats_ready"), sem("rstd_ready"), sem("normed")
        full = [sem("full0"), sem("full1")]
        freed = [sem("freed0"), sem("freed1")]
        er_ready = sem("er_ready")
        exponents_ready, exps_ready, rwkv_ready = sem("exponents_ready"), sem("exps_ready"), sem("rwkv_ready")
        mixing_read = sem("mixing_read")
        ctx4_ready, context_ready = sem("ctx4_ready"), sem("context_ready")
        scores_full, scores_read = sem("scores_full"), sem("scores_read")
        exp_ready, probs_turned, probT_ready = sem("exp_ready"), sem("probs_turned"), sem("probT_ready")
        heads_ready = sem("heads_ready")
        gates_ready = sem("gates_ready")
        hi_ready, lo_ready = sem("hi_ready"), sem("lo_ready")
        z_full, hid_ready, hid_used = sem("z_full"), sem("hid_ready"), sem("hid_used")
        y_full, y_ready = sem("y_full"), sem("y_ready")
        stored = sem("stored")

        def part(name):
            return pk[:, PACK[name][0]:PACK[name][1]]

        ident = part("ident")
        cols = part("cols")
        first = cols[:, 1:2]

        def now(t):
            return t.rearrange("p (b t) -> p b t", t=TP)[:, :, 1:TP]

        def before(t):
            return t.rearrange("p (b t) -> p b t", t=TP)[:, :, 0:T]

        def pads(t):
            return t.rearrange("p (b t) -> p b t", t=TP)[:, :, 0:1]

        def by_batch(t):
            return t.rearrange("p (b t) -> p b t", t=T)

        def shared_bank(st):
            return bank_m[shared[st] % 2]

        def wait_full(eng, st):
            eng.wait_ge(full[shared[st] % 2], shared[st] // 2 + 1)

        def wait_moved(eng, st):
            eng.wait_ge(freed[shared[st] % 2], shared[st] // 2 + 1)

        def wait_bank(eng, st):
            if shared[st] >= 2:
                eng.wait_ge(freed[shared[st] % 2], shared[st] // 2)

        def fill_done(ins, st):
            ins.then_inc(full[shared[st] % 2], 1)

        def moved(ins, st):
            ins.then_inc(freed[shared[st] % 2], 1)

        def wait_down(eng, i):
            if i % FT == FT - 1:
                eng.wait_ge(y_full, i // FT + 1)
            else:
                eng.wait_ge(hid_used, i // FT * (FT - 1) + i % FT + 1)

        def batches(g, b):
            return range(GB * g, GB * g + GB) if b is None else range(GB * g + b, GB * g + b + 1)

        block = ctx.enter_context(nc.Block())

        @block.sync
        def _(sp):
            sp.dma_start(resid[:, 0:GB, :], x[:, 0:GB, :]).then_inc(x_in[0], 16)
            sp.dma_start(pk[:, :], pack).then_inc(pack_in, 16)
            sp.dma_start(w96[:, :], wkv96).then_inc(ctx_in, 16)
            sp.dma_start(ctx_sb[:, :, :], ctxT).then_inc(ctx_in, 16)
            sp.dma_start(br_sb[:, :], br).then_inc(small_in, 16)
            for q in range(NQ):
                sp.dma_start(mask_u8[32 * q:32 * q + 1, :], mask).then_inc(small_in, 16)
            for g in range(1, G):
                sp.dma_start(resid[:, GB * g:GB * g + GB, :], x[:, GB * g:GB * g + GB, :]).then_inc(x_in[g], 16)
            for e in range(E):
                if e >= 2:
                    sp.wait_ge(w1_split, e - 1)
                sp.dma_start(w1_raw[:, e % 2, :], w1[:, e * F:(e + 1) * F]).then_inc(w1_in[e], 16)
                if e == 1:
                    sp.dma_start(w2_sb[:, :], w2).then_inc(w2_in, 16)
            for g in range(G):
                wait_moved(sp, ("gated", g, E - 1))
                sp.dma_start(out[:, GB * g:GB * g + GB, :], resid[:, GB * g:GB * g + GB, :]).then_inc(stored, 16)
            sp.wait_ge(stored, 16 * G)

        @block.gpsimd
        def _(pool):
            chain = [0]

            def link(ins):
                chain[0] += 1
                ins.then_inc(pool_step, 1)
                pool.wait_ge(pool_step, chain[0])

            nc.gpsimd.memset(half_neg[:, :], -0.5)
            nc.gpsimd.memset(xT1[:, :, :], 0.0)
            nc.gpsimd.memset(ex[:, :, :], 0.0)
            nc.gpsimd.memset(v_sb[:, :], 0.0)
            nc.gpsimd.memset(ev[:, :], 0.0)
            nc.gpsimd.memset(k_sb[:, :], NEG)
            nc.gpsimd.memset(prob[:, :, :], 0.0)
            nc.gpsimd.memset(ctx4[:, :, :], 0.0)
            nc.gpsimd.memset(ones_b[:, :], 1.0)
            link(nc.gpsimd.memset(ones_f[:, :], 1.0))
            nc.gpsimd.memset(var_e[:, :, :], 1.0).then_inc(pool_const, 1)

            def split_w1(e):
                pool.wait_ge(w1_in[e], 16)
                hi, raw = w1_hi[:, e * F:(e + 1) * F], w1_raw[:, e % 2, :]
                link(nc.gpsimd.tensor_copy(hi, raw))
                nc.gpsimd.tensor_tensor(w1_lo[:, e * F:(e + 1) * F], raw, hi.bitcast(F32), ALU.subtract)\
                    .then_inc(w1_split, 1)

            def stats(st):
                _, k, g, b = st
                pool.wait_ge(stats_ready, nth[st])
                at = batches(g, b)
                lo, hi = at[0], at[-1] + 1
                v = var_e[:, k, lo:hi]
                link(nc.gpsimd.tensor_scalar(v, mv[:, k, lo:hi, 1], EPS, 1.0, ALU.add, ALU.mult))
                nc.gpsimd.tensor_tensor(rstd[:, k, lo:hi], v, half_neg[:, 0:hi - lo], ALU.pow)\
                    .then_inc(rstd_ready, 1)

            def replicate(i):
                if i == 0:
                    pool.wait_ge(ctx_in, 32)
                if i >= 2:
                    j = ("context", (i - 2) // GB, (i - 2) % GB)
                    wait_full(pool, j)
                nc.gpsimd.tensor_copy(ctx4[:, i % 2, 0:SQ].rearrange("p (h m) -> p h m", m=M),
                                      ctx_sb[:, i:i + 1, :].broadcast_to([CTX, QH, M]))\
                    .then_inc(ctx4_ready, 1)

            early = 0
            for st in steps:
                if st[0] == "stats":
                    stats(st)
                if st[0] == "stats" and st[1] == 0 and st[2] == 0:
                    replicate(0)
                    replicate(1)
                if st[0] == "context" and GB * st[1] + st[2] + 2 < B:
                    replicate(GB * st[1] + st[2] + 2)
                if st[0] in ("key", "scores") and early < E:
                    split_w1(early)
                    early += 1

        @block.scalar
        def _(act):
            act.wait_ge(pack_in, 16)
            nc.scalar.activation(decay_w[:, :], cols[:, 0:1], ACT.Exp).then_inc(act_const, 1)
            act.wait_ge(pool_const, 1)

            def turn(st):
                _, k, g, b = st
                wait_full(act, st)
                src = shared_bank(st)
                if k == 0:
                    if g >= 2:
                        wait_full(act, ("receptance", g - 2))
                    moved(nc.scalar.activation(now(xT1[:, g % 2, :]), by_batch(src[:, :]), ACT.Copy), st)
                elif k == 1:
                    if g >= 1:
                        wait_full(act, ("query", g - 1))
                    moved(nc.scalar.activation(xT2[:, :], src[:, :], ACT.Copy), st)
                else:
                    at = slice(b * T, b * T + T)
                    if g >= 1:
                        wait_full(act, ("router", g - 1))
                    if g >= 2:
                        act.wait_ge(z_full, NS * (g - 1))
                    nc.scalar.activation(x_hi[:, g % 2, at], src[:, 0:T], ACT.Copy).then_inc(hi_ready, 1)
                    moved(nc.scalar.activation(xT3[:, at], src[:, 0:T], ACT.Copy), st)

            def key(st):
                g = st[1]
                wait_full(act, st)
                if g >= 1:
                    act.wait_ge(mixing_read, g)
                moved(nc.scalar.activation(now(k_sb[:, :]), by_batch(shared_bank(st)[:, :]), ACT.Copy), st)

            def value(st):
                wait_full(act, st)
                moved(nc.scalar.activation(now(v_sb[:, :]), by_batch(shared_bank(st)[:, :]), ACT.Copy), st)

            def receptance(st):
                wait_full(act, st)
                moved(nc.scalar.activation(er[:, :], shared_bank(st)[:, :], ACT.Exp, scale=-1.0), st)

            def decay(st):
                g = st[1]
                for i in range(2):
                    act.wait_ge(exponents_ready, 2 * g + i + 1)
                    part2 = ex[:, 2 * i:2 * i + 2, :].rearrange("p e (b t) -> p e b t", t=TP)[:, :, :, 1:TP]
                    nc.scalar.activation(part2, part2, ACT.Exp).then_inc(exps_ready, 1)

            def query(st):
                g = st[1]
                wait_full(act, st)
                if g >= 2:
                    act.wait_ge(scores_full, UNITS * (g - 1))
                moved(nc.scalar.activation(qT[:, g % 2, :], shared_bank(st)[:, :], ACT.Copy), st)

            def scores(st):
                u = nth[st] - 1
                act.wait_ge(scores_read, u + 1)
                pr = prob[:, u % 3, 0:SQ]
                nc.scalar.activation(pr, pr, ACT.Exp).then_inc(exp_ready, 1)

            def turn_probs(st):
                u = nth[st] - 1
                act.wait_ge(probs_turned, u + 1)
                if u >= 2:
                    wait_full(act, ("probs_v", (u - 2) // UNITS, (u - 2) % UNITS))
                nc.scalar.activation(probT[:, u % 2, :], bank_p[:, 0:SP], ACT.Copy).then_inc(probT_ready, 1)

            def turn_heads(st):
                i = nth[st] - 1
                wait_full(act, st)
                if i >= 2:
                    wait_full(act, ("attended", (i - 2) // GB, (i - 2) % GB))
                moved(nc.scalar.activation(headsT[:, i % 2, :], shared_bank(st)[:, 0:C], ACT.Copy), st)

            def router(st):
                g = st[1]
                wait_full(act, st)
                if g >= 1:
                    act.wait_ge(gates_ready, g)
                moved(nc.scalar.activation(xs[:, :, :], shared_bank(st)[:, 0:GB * E]
                                           .rearrange("p (b e) -> p b e", e=E), ACT.Copy, scale=0.5), st)

            def hidden(st):
                i, s = nth[st] - 1, st[2]
                act.wait_ge(z_full, i + 1)
                if i >= 3:
                    wait_down(act, i - 3)
                nc.scalar.activation(hid[:, i % 3, :], bank_z[i % 2][:, :], ACT.Relu,
                                     bias=part("b1")[:, s:s + 1]).then_inc(hid_ready, 1)

            def down(st):
                _, g, s = st
                if s % FT < FT - 1:
                    return
                e = s // FT
                i = E * g + e
                act.wait_ge(y_full, i + 1)
                if i >= 2:
                    wait_full(act, ("gated", (i - 2) // E, (i - 2) % E))
                nc.scalar.activation(yT[:, i % 2, :], bank_y[:, :], ACT.Identity,
                                     bias=part("b2")[:, e:e + 1]).then_inc(y_ready, 1)

            run = {"turn": turn, "key": key, "value": value, "receptance": receptance, "decay": decay,
                   "query": query, "scores": scores, "turn_probs": turn_probs, "turn_heads": turn_heads,
                   "router": router, "hidden": hidden, "down": down}
            for st in steps:
                if st[0] in run:
                    run[st[0]](st)

        @block.vector
        def _(dve):
            chain = [0]

            def link(ins):
                chain[0] += 1
                ins.then_inc(dve_step, 1)
                dve.wait_ge(dve_step, chain[0])

            v = nc.vector
            v.memset(decay_row[:, :], 0.0).then_inc(dve_step, 1)
            chain[0] += 1
            dve.wait_ge(pack_in, 16)
            dve.wait_ge(pool_const, 1)
            link(v.tensor_scalar(mix_c[:, :], cols[:, 2:5], -1.0, 1.0, ALU.mult, ALU.add))
            for i, name in enumerate(("wkT", "wvT", "wrT")):
                v.tensor_scalar(w_now[:, i, :], part(name), cols[:, 2 + i:3 + i], None, ALU.mult)
                ins = v.tensor_scalar(w_before[:, i, :], part(name), mix_c[:, i:i + 1], None, ALU.mult)
            ins.then_inc(dve_const, 1)
            dve.wait_ge(act_const, 1)
            v.tensor_scalar(now(decay_row[:, :]), now(decay_row[:, :]), decay_w[:, 0:1], None, ALU.subtract)\
                .then_inc(dve_step, 1)
            v.memset(pads(decay_row[:, :]), NEG).then_inc(dve_step, 1)
            chain[0] += 2

            def consts():
                dve.wait_ge(small_in, 16 * (NQ + 1))
                for q in range(NQ):
                    v.tensor_scalar(mask_bias[32 * q:32 * q + 1, :, :].rearrange("p b m -> p (b m)"),
                                    mask_u8[32 * q:32 * q + 1, :], -1.0, MASKED, ALU.add, ALU.mult)\
                        .then_inc(dve_const, 1)
                for i in range(2):
                    v.tensor_copy(vbd[:, i, :].rearrange("p (k d) -> p k d", d=HD + 1)[:, :, HD], part("vmask"))

            def stats(st):
                _, k, g, b = st
                if k == 0:
                    dve.wait_ge(x_in[g], 16)
                for i in batches(g, b):
                    ins = v.bn_stats(bn[:, i, :], resid[:, i, :])
                link(ins)
                for i in batches(g, b):
                    ins = v.bn_aggr(mv[:, k, i, :], bn[:, i, :])
                ins.then_inc(stats_ready, 1)

            def norm(st):
                _, k, g, b = st
                dve.wait_ge(rstd_ready, nth[st])
                for i in batches(g, b):
                    ins = v.tensor_scalar(xn[:, i, :], resid[:, i, :], mv[:, k, i, 0:1], rstd[:, k, i:i + 1],
                                          ALU.subtract, ALU.mult)
                ins.then_inc(normed, 1)

            def turn(st):
                _, k, g, b = st
                if k == 2:
                    wait_moved(dve, st)
                    if g >= 2:
                        dve.wait_ge(z_full, NS * (g - 1))
                    at = slice(b * T, b * T + T)
                    v.tensor_tensor(x_lo[:, g % 2, at], xT3[:, at], x_hi[:, g % 2, at].bitcast(F32),
                                    ALU.subtract).then_inc(lo_ready, 1)

            mst = now(mx[:, :])

            def decay(st):
                g = st[1]
                wait_moved(dve, ("key", g))
                if g == 0:
                    dve.wait_ge(dve_step, chain[0])
                link(v.tensor_tensor_scan(mx[:, :], decay_row[:, :], k_sb[:, :], NEG, ALU.add, ALU.max))
                e = [now(ex[:, i, :]) for i in range(4)]
                kk, old = now(k_sb[:, :]), before(mx[:, :])
                v.scalar_tensor_tensor(e[0], old, decay_w[:, 0:1], mst, ALU.subtract, ALU.subtract)
                v.tensor_tensor(e[1], kk, mst, ALU.subtract).then_inc(exponents_ready, 1)
                link(v.scalar_tensor_tensor(by_batch(ta[:, :]), kk, first, old, ALU.add, ALU.subtract))
                v.tensor_scalar(e[2], by_batch(ta[:, :]), -1.0, 0.0, ALU.mult, ALU.min)
                v.tensor_scalar(e[3], by_batch(ta[:, :]), 0.0, None, ALU.min).then_inc(exponents_ready, 1)

            def scans(st):
                g = st[1]
                dve.wait_ge(exps_ready, 2 * g + 1)
                wait_moved(dve, ("value", g))
                link(v.tensor_tensor(now(ev[:, :]), now(ex[:, 1, :]), now(v_sb[:, :]), ALU.mult))
                v.tensor_tensor_scan(den[:, :], ex[:, 0, :], ex[:, 1, :], 0.0, ALU.mult, ALU.add)
                link(v.tensor_tensor_scan(num[:, :], ex[:, 0, :], ev[:, :], 0.0, ALU.mult, ALU.add))

            def mix(st):
                g = st[1]
                dve.wait_ge(exps_ready, 2 * g + 2)
                a, b_, c = by_batch(ta[:, :]), by_batch(tb[:, :]), by_batch(tc[:, :])
                v.tensor_tensor(a, now(ex[:, 2, :]), before(num[:, :]), ALU.mult)
                v.tensor_tensor(b_, now(ex[:, 3, :]), now(v_sb[:, :]), ALU.mult)
                link(v.tensor_tensor(c, now(ex[:, 2, :]), before(den[:, :]), ALU.mult))
                v.tensor_tensor(ta[:, :], ta[:, :], tb[:, :], ALU.add)
                link(v.tensor_tensor(c, c, now(ex[:, 3, :]), ALU.add))
                wait_moved(dve, ("receptance", g))
                v.scalar_tensor_tensor(tb[:, :], er[:, :], 1.0, tc[:, :], ALU.add, ALU.mult)\
                    .then_inc(mixing_read, 1)

            def rwkv_(st):
                g = st[1]
                dve.wait_ge(mixing_read, g + 1)
                link(v.reciprocal(tc[:, :], tb[:, :]))
                if g >= 1:
                    wait_full(dve, ("mixed", g - 1))
                v.tensor_tensor(rwkv[:, :], ta[:, :], tc[:, :], ALU.mult).then_inc(rwkv_ready, 1)

            def mixed(st):
                g = st[1]
                wait_full(dve, st)
                r = resid[:, GB * g:GB * g + GB, :]
                moved(v.tensor_tensor(r, r, by_batch(shared_bank(st)[:, :]), ALU.add), st)
                wait_moved(dve, st)

            def context(st):
                i = nth[st] - 1
                if i == 0:
                    consts()
                wait_full(dve, st)
                if i >= 2:
                    j = i - 2
                    wait_full(dve, ("probs_v", j // GB, NQ * (j % GB) + NQ - 1))
                src = shared_bank(st)
                v.tensor_tensor(kbd[:, i % 2, :].rearrange("p (h m) -> p h m", m=M),
                                src[:, 0:M].rearrange("p (o m) -> p o m", o=1).broadcast_to([P, QH, M]),
                                part("qmask").rearrange("p (h o) -> p h o", o=1).broadcast_to([P, QH, M]),
                                ALU.mult).then_inc(context_ready, 1)
                moved(v.tensor_tensor(
                    vbd[:, i % 2, :].rearrange("p (k d) -> p k d", d=HD + 1)[:, :, 0:HD],
                    src[:, P:P + KT * C].rearrange("p (k d) -> p k d", d=HD),
                    part("vmask").rearrange("p (k o) -> p k o", o=1).broadcast_to([P, KT * H, HD]),
                    ALU.mult), st)

            def scores(st):
                u = nth[st] - 1
                dve.wait_ge(scores_full, u + 1)
                s = bank_s[u % 2][:, 0:SQ].rearrange("p (h m) -> p h m", m=M)
                link(v.tensor_reduce(smax[:, u % 2, :], s, AX_X, ALU.max))
                if u >= 3:
                    dve.wait_ge(probs_turned, u - 2)
                v.tensor_tensor(prob[:, u % 3, 0:SQ].rearrange("p (h m) -> p h m", m=M), s,
                                smax[:, u % 2, :].rearrange("p (h o) -> p h o", o=1).broadcast_to([P, QH, M]),
                                ALU.subtract).then_inc(scores_read, 1)

            def probs_v(st):
                _, g, u = st
                wait_full(dve, st)
                o = shared_bank(st)[:, 0:QH * (HD + 1)].rearrange("p (h d) -> p h d", d=HD + 1)
                i = GB * g + u // NQ
                rs = rsum[:, u % 2, :].rearrange("p (h o) -> p h o", o=1)
                link(v.reciprocal(rs, o[:, :, HD:HD + 1]))
                if u % NQ == 0 and i >= 2:
                    wait_full(dve, ("turn_heads", (i - 2) // GB, (i - 2) % GB))
                q = u % NQ
                moved(v.tensor_tensor(heads[:, i % 2, q * QH * HD:(q + 1) * QH * HD]
                                      .rearrange("p (h d) -> p h d", d=HD),
                                      o[:, :, 0:HD], rs.broadcast_to([P, QH, HD]), ALU.mult), st)

            def attended(st):
                _, g, b = st
                wait_full(dve, st)
                r = resid[:, GB * g + b, :]
                moved(v.tensor_tensor(r, r, shared_bank(st)[:, 0:C], ALU.add), st)
                wait_moved(dve, st)

            def router(st):
                g = st[1]
                wait_moved(dve, st)

                def wide(t):
                    return t.rearrange("p (b o) -> p b o", o=1).broadcast_to([P, GB, E])

                link(v.tensor_reduce(top[:, :], xs[:, :, :], AX_X, ALU.max))
                link(v.tensor_tensor(xs[:, :, :], xs[:, :, :], wide(top[:, :]), ALU.subtract))
                link(v.memset(tau[:, :], -1.0))

                def above():
                    link(v.tensor_tensor(t8a[:, :, :], xs[:, :, :], wide(tau[:, :]), ALU.subtract))
                    v.scalar_tensor_tensor(t8b[:, :, :], t8a[:, :, :], 0.0, t8a[:, :, :], ALU.max, ALU.mult)
                    link(v.tensor_scalar(t8a[:, :, :], t8a[:, :, :], 0.0, None, ALU.max))
                    link(v.tensor_reduce(s2[:, :], t8b[:, :, :], AX_X, ALU.add))

                for _ in range(NEWTON):
                    above()
                    link(v.tensor_reduce(s1[:, :], t8a[:, :, :], AX_X, ALU.add))
                    link(v.reciprocal(s1[:, :], s1[:, :]))
                    link(v.scalar_tensor_tensor(s2[:, :], s2[:, :], -1.0, s1[:, :], ALU.add, ALU.mult))
                    link(v.scalar_tensor_tensor(tau[:, :], s2[:, :], 0.5, tau[:, :], ALU.mult, ALU.add))
                above()
                link(v.reciprocal(s2[:, :], s2[:, :]))
                link(v.tensor_tensor(t8a[:, :, :], t8b[:, :, :], wide(s2[:, :]), ALU.mult))
                v.scalar_tensor_tensor(gates[:, g % 2, :, :], t8a[:, :, :], THRESH, t8a[:, :, :],
                                       ALU.is_gt, ALU.mult).then_inc(gates_ready, 1)

            def gated(st):
                _, g, e = st
                if e == 0:
                    dve.wait_ge(gates_ready, g + 1)
                wait_full(dve, st)
                if e > 0:
                    wait_moved(dve, ("gated", g, e - 1))
                src = shared_bank(st)
                for b in range(GB):
                    r = resid[:, GB * g + b, :]
                    ins = v.scalar_tensor_tensor(r, src[:, b * C:(b + 1) * C], gates[:, g % 2, b, e:e + 1], r,
                                                 ALU.mult, ALU.add)
                moved(ins, st)

            run = {"stats": stats, "norm": norm, "turn": turn, "decay": decay, "scans": scans, "mix": mix,
                   "rwkv": rwkv_, "mixed": mixed, "context": context, "scores": scores, "probs_v": probs_v,
                   "attended": attended, "router": router, "gated": gated}
            for st in steps:
                if st[0] in run:
                    run[st[0]](st)

        @block.tensor
        def _(pe):
            mm = nc.tensor.matmul
            pe.wait_ge(pack_in, 16)
            pe.wait_ge(dve_const, 1)
            pe.wait_ge(pool_const, 1)

            def turn(st):
                _, k, g, b = st
                pe.wait_ge(normed, nth[st])
                wait_bank(pe, st)
                for n, i in enumerate(batches(g, b)):
                    ins = nc.tensor.transpose(shared_bank(st)[:, n * T:(n + 1) * T], xn[:, i, :], ident)
                fill_done(ins, st)

            def project(st, i):
                g = st[1]
                wait_moved(pe, ("turn", 0, g, None))
                wait_bank(pe, st)
                dst = by_batch(shared_bank(st)[:, :])
                mm(dst, w_now[:, i, :], now(xT1[:, g % 2, :]), start=True, stop=False)
                fill_done(mm(dst, w_before[:, i, :], before(xT1[:, g % 2, :]), start=False, stop=True), st)

            def mixed(st):
                g = st[1]
                pe.wait_ge(rwkv_ready, g + 1)
                wait_bank(pe, st)
                for b in range(GB):
                    ins = mm(shared_bank(st)[:, b * C:(b + 1) * C], rwkv[:, b * T:(b + 1) * T], part("woT"),
                             start=True, stop=True)
                fill_done(ins, st)

            def query(st):
                wait_moved(pe, ("turn", 1, st[1], None))
                wait_bank(pe, st)
                fill_done(mm(shared_bank(st)[:, :], part("Wq"), xT2[:, :], start=True, stop=True), st)

            def context(st):
                i = nth[st] - 1
                if i == 0:
                    pe.wait_ge(ctx_in, 32)
                pe.wait_ge(ctx4_ready, i + 1)
                wait_bank(pe, st)
                dst = shared_bank(st)
                mm(dst[:, 0:M], w96[:, 0:C], ctx_sb[:, i, :], start=True, stop=True)
                for k in range(KT):
                    ins = mm(dst[:, P + k * C:P + (k + 1) * C], ctx4[:, i % 2, k * P:(k + 1) * P],
                             w96[:, C:2 * C], start=True, stop=True)
                fill_done(ins, st)

            def scores(st):
                _, g, u = st
                b, q = u // NQ, u % NQ
                i = GB * g + b
                n = nth[st] - 1
                if u == 0:
                    wait_moved(pe, ("query", g))
                if q == 0:
                    pe.wait_ge(context_ready, i + 1)
                if n == 0:
                    pe.wait_ge(dve_const, 1 + NQ)
                if n >= 2:
                    pe.wait_ge(scores_read, n - 1)
                rows = slice(32 * q, 32 * q + 32)
                dst = bank_s[n % 2][:, 0:SQ]
                mm(dst, qT[rows, g % 2, b * T:(b + 1) * T], kbd[rows, i % 2, :], start=True, stop=False)
                mm(dst.rearrange("p (h m) -> p h m", m=M), ones_b[32 * q:32 * q + 1, :],
                   mask_bias[32 * q:32 * q + 1, i:i + 1, :].broadcast_to([1, QH, M]),
                   start=False, stop=True).then_inc(scores_full, 1)

            def turn_probs(st):
                n = nth[st] - 1
                pe.wait_ge(exp_ready, n + 1)
                if n >= 1:
                    pe.wait_ge(probT_ready, n)
                for k in range(KT):
                    ins = nc.tensor.transpose(bank_p[:, k * P:(k + 1) * P], prob[:, n % 3, k * P:(k + 1) * P],
                                              ident)
                ins.then_inc(probs_turned, 1)

            def probs_v(st):
                _, g, u = st
                n = nth[st] - 1
                i, q = n // NQ, n % NQ
                pe.wait_ge(probT_ready, n + 1)
                if q == 0:
                    wait_moved(pe, ("context", g, u // NQ))
                wait_bank(pe, st)
                w = QH * (HD + 1)
                for k in range(KT):
                    at = (k * H + q * QH) * (HD + 1)
                    ins = mm(shared_bank(st)[:, 0:w], probT[:, n % 2, k * P:(k + 1) * P],
                             vbd[:, i % 2, at:at + w], start=(k == 0), stop=(k == KT - 1))
                fill_done(ins, st)

            def turn_heads(st):
                _, g, b = st
                i = nth[st] - 1
                wait_moved(pe, ("probs_v", g, NQ * b + NQ - 1))
                wait_moved(pe, ("probs_v", g, NQ * b + NQ - 2))
                wait_bank(pe, st)
                fill_done(nc.tensor.transpose(shared_bank(st)[:, 0:T], heads[:, i % 2, :], ident), st)

            def attended(st):
                i = nth[st] - 1
                wait_moved(pe, ("turn_heads", st[1], st[2]))
                wait_bank(pe, st)
                fill_done(mm(shared_bank(st)[:, 0:C], headsT[:, i % 2, :], part("Wo"), start=True, stop=True), st)

            def router(st):
                g = st[1]
                for b in range(GB):
                    wait_moved(pe, ("turn", 2, g, b))
                wait_bank(pe, st)
                for b in range(GB):
                    dst = shared_bank(st)[:, b * E:(b + 1) * E]
                    mm(dst, xT3[:, b * T:(b + 1) * T], part("Wr"), start=True, stop=False)
                    ins = mm(dst, ones_f[0:1, :], br_sb[0:1, :], start=False, stop=True)
                fill_done(ins, st)

            def hidden(st):
                _, g, s = st
                n = nth[st] - 1
                if s == 0:
                    pe.wait_ge(hi_ready, GB * (g + 1))
                    pe.wait_ge(lo_ready, GB * (g + 1))
                if g == 0 and s % FT == 0:
                    pe.wait_ge(w1_split, s // FT + 1)
                if n >= 2:
                    pe.wait_ge(hid_ready, n - 1)
                at = slice(s * P, (s + 1) * P)
                z = bank_z[n % 2][:, :]
                mm(z, w1_lo[:, at], x_hi[:, g % 2, :], start=True, stop=False)
                mm(z, w1_hi[:, at], x_lo[:, g % 2, :], start=False, stop=False)
                mm(z, w1_hi[:, at], x_hi[:, g % 2, :], start=False, stop=True).then_inc(z_full, 1)

            def down(st):
                _, g, s = st
                n = nth[st] - 1
                if n == 0:
                    pe.wait_ge(w2_in, 16)
                pe.wait_ge(hid_ready, n + 1)
                if s % FT == 0 and n > 0:
                    pe.wait_ge(y_ready, n // FT)
                ins = mm(bank_y[:, :], w2_sb[:, s * C:(s + 1) * C], hid[:, n % 3, :],
                         start=(s % FT == 0), stop=(s % FT == FT - 1))
                if s % FT == FT - 1:
                    ins.then_inc(y_full, 1)
                else:
                    ins.then_inc(hid_used, 1)

            def gated(st):
                n = nth[st] - 1
                pe.wait_ge(y_ready, n + 1)
                wait_bank(pe, st)
                for b in range(GB):
                    ins = nc.tensor.transpose(shared_bank(st)[:, b * C:(b + 1) * C],
                                              yT[:, n % 2, b * T:(b + 1) * T], ident)
                fill_done(ins, st)

            run = {"turn": turn, "key": lambda st: project(st, 0), "value": lambda st: project(st, 1),
                   "receptance": lambda st: project(st, 2), "mixed": mixed, "query": query,
                   "context": context, "scores": scores, "turn_probs": turn_probs, "probs_v": probs_v,
                   "turn_heads": turn_heads, "attended": attended, "router": router, "hidden": hidden,
                   "down": down, "gated": gated}
            for st in steps:
                if st[0] in run:
                    run[st[0]](st)


def kernel(x, ctx_768, mask_BxS2_bf1, L0_attn_wk, L0_attn_wv, L0_attn_wr, L0_attn_wo, L0_attn_time_decay,
           L0_attn_time_first, L0_attn_mix_k, L0_attn_mix_v, L0_attn_mix_r, L0_xattn_Wq, L0_xattn_Wk,
           L0_xattn_Wv, L0_xattn_Wo, L0_ffn_Wr, L0_ffn_br, L0_ffn_W1, L0_ffn_b1, L0_ffn_W2, L0_ffn_b2):
    import numpy as np
    import concourse.bacc as bacc
    from concourse.bass_utils import run_bass_kernel_spmd

    f32 = np.float32
    ident = np.eye(P, dtype=f32)
    c, h = np.arange(P)[:, None], np.arange(QH)[None, :]
    qmask = ((c // HD) % QH == h).astype(f32) * f32(HD ** -0.5)
    r = np.arange(KT * P).reshape(KT, P).T[:, :, None]
    vmask = (r // M == np.arange(H)[None, None, :] % QH).astype(f32).reshape(P, KT * H)
    cols = np.stack([np.asarray(a).reshape(C) for a in
                     (L0_attn_time_decay, L0_attn_time_first, L0_attn_mix_k, L0_attn_mix_v, L0_attn_mix_r)], 1)
    b1 = np.asarray(L0_ffn_b1).reshape(NS, P).T
    pack = np.concatenate([ident, qmask, vmask, cols, np.asarray(L0_attn_wk).T, np.asarray(L0_attn_wv).T,
                           np.asarray(L0_attn_wr).T, np.asarray(L0_attn_wo).T, np.asarray(L0_xattn_Wq),
                           np.asarray(L0_xattn_Wo), np.asarray(L0_ffn_Wr), b1, np.asarray(L0_ffn_b2).T], 1)
    arrays = {
        "x": np.asarray(x).transpose(1, 0, 2),
        "ctxT": np.asarray(ctx_768).transpose(2, 0, 1),
        "mask": np.asarray(mask_BxS2_bf1).reshape(1, B * M).view(np.uint8),
        "pack": pack,
        "wkv96": np.concatenate([np.asarray(L0_xattn_Wk), np.asarray(L0_xattn_Wv)], 1),
        "br": np.asarray(L0_ffn_br).reshape(1, E),
        "w1": np.asarray(L0_ffn_W1).transpose(1, 0, 2).reshape(P, E * F),
        "w2": np.asarray(L0_ffn_W2).reshape(NS, P, C).transpose(1, 0, 2).reshape(P, NS * C),
    }
    arrays = {n: np.ascontiguousarray(a) for n, a in arrays.items()}
    nc = bacc.Bacc("TRN2", target_bir_lowering=False, num_devices=1)
    args = [nc.dram_tensor(n, a.shape, mybir.dt.from_np(a.dtype), kind="ExternalInput").ap()
            for n, a in arrays.items()]
    args.append(nc.dram_tensor("out", (T, B, C), F32, kind="ExternalOutput").ap())
    build(nc, *args)
    got = run_bass_kernel_spmd(nc, [arrays], core_ids=[0]).results[0]["out"]
    return np.ascontiguousarray(got.transpose(1, 0, 2))
```

```python
from contextlib import ExitStack

import concourse.bass as bass
from concourse import mybir

F32 = mybir.dt.float32
F32R = mybir.dt.float32r
BF16 = mybir.dt.bfloat16
U8 = mybir.dt.uint8
ALU = mybir.AluOpType
ACT = mybir.ActivationFunctionType
AX_X = mybir.AxisListType.X

P = 128
B, T, C = 16, 128, 128
SIZES = (4, 4, 4, 4)
G = len(SIZES)
START = [sum(SIZES[:g]) for g in range(G)]
GB = max(SIZES)
N = GB * T
TP = T + 1
NPAD = GB * TP
M, CTX = 77, 96
H, HD = 16, 8
QH = 4
NQ = H // QH
SQ = QH * M
KT = -(-SQ // P)
SP = KT * P
E, F = 8, 512
FT = F // P
NS = E * FT
NEWTON = 6
RAW = 4
CTX_RING = 4
PROBS = 4
EPS = 1e-5
THRESH = 1e-9
NEG = -1e38
MASKED = 3.3895313892515355e38

PACK = {}
_at = 0
for _name, _n in (("ident", P), ("qmask", QH), ("vmask", KT * H), ("cols", 5), ("wkT", C), ("wvT", C),
                  ("wrT", C), ("woT", C), ("Wq", C), ("Wo", C), ("Wr", E), ("b1", NS), ("b2", E)):
    PACK[_name] = (_at, _at + _n)
    _at += _n
PACKED = _at


def mixing_steps(g, t):
    n = SIZES[g]
    norm = [[("norm", k, g, b) for b in range(n)] for k in range(2)]
    return {
        0: [("stats", 0, g, None)],
        2: norm[0][0:2],
        3: norm[0][2:n],
        4: [("turn", 0, g, None)],
        5: [("key", g)],
        6: [("value", g), ("maximum", g)],
        7: [("receptance", g), ("exponent", g, 0), ("exponent", g, 1)],
        8: [("exponent", g, 2), ("exp", g, 0)],
        9: [("exponent", g, 3), ("exp", g, 1)],
        10: [("weighted", g), ("exp", g, 2)],
        11: [("scan_den", g), ("exp", g, 3)],
        12: [("scan_num", g), ("denominator", g)],
        14: [("numerator", g, 0)],
        16: [("numerator", g, 1)],
        17: [("receive", g)],
        18: [("inverse", g, 0)],
        19: [("inverse", g, 1)],
        20: [("inverse", g, 2)],
        21: [("inverse", g, 3)],
        22: [("rwkv", g)],
        24: [("mixed", g)],
        25: [("stats", 1, g, None)],
        27: norm[1][0:2],
        28: norm[1][2:n],
        29: [("turn", 1, g, None)],
        31: [("query", g)],
    }.get(t, [])


MIXING_TICKS = 32


def attention_steps(g, t):
    out = []
    units = NQ * SIZES[g]
    if 0 <= t - 5 < units:
        out.append(("probs_v", g, t - 5))
    if t % NQ == 0 and t < units:
        out.append(("context", g, t // NQ))
    if 0 <= t - 1 < units:
        out.append(("scores", g, t - 1))
    if 0 <= t - 3 < units:
        out.append(("turn_probs", g, t - 3))
    for after, what in ((10, [("turn_heads", g)]), (12, [("attended", g), ("stats", 2, g)]),
                        (14, [("norm", 2, g)]), (15, [("turn", 2, g)])):
        b, rest = divmod(t - after, NQ)
        if rest == 0 and 0 <= b < SIZES[g]:
            out += [(*w, b) for w in what]
    if t == units + 13:
        out.append(("router", g))
    if 0 <= t - units - 14 <= NEWTON:
        out.append(("threshold", g, t - units - 14))
    return out


DOWN_LAG, GATE_LAG = 2, 8
EXPERT_TICKS = NS + GATE_LAG - FT + 1


def expert_steps(g, t):
    out = []
    if 0 <= t - DOWN_LAG < NS:
        out.append(("down", g, t - DOWN_LAG))
    if t < NS:
        out.append(("hidden", g, t))
    e, rest = divmod(t - GATE_LAG, FT)
    if rest == 0 and 0 <= e < E:
        out.append(("gated", g, e))
    if t == EXPERT_TICKS - 1:
        out.append(("store", g))
    return out


SPLIT_AT = (9, 13, 15, 17, 19, 21, 23, 29)
ORDER = {k: i for i, k in enumerate(("down", "probs_v", "context", "hidden", "scores", "turn_probs", "others",
                                      "gated", "store"))}


def plan():
    mixing_at, attention_at, experts_at = {0: 0}, {0: MIXING_TICKS}, {}
    mixing_at[1] = MIXING_TICKS
    at = MIXING_TICKS + max(NQ * SIZES[0] + 14, MIXING_TICKS)
    for g in range(G):
        experts_at[g] = at
        attention_at[g + 1], mixing_at[g + 2] = at, at
        at += NS
    steps = []
    for t in range(at + EXPERT_TICKS - NS):
        tick = [("split", e) for e in range(E) if t == SPLIT_AT[e]]
        for g in range(G):
            if 0 <= t - experts_at[g] < EXPERT_TICKS:
                tick += expert_steps(g, t - experts_at[g])
            if t >= attention_at[g]:
                tick += attention_steps(g, t - attention_at[g])
            if t >= mixing_at[g]:
                tick += mixing_steps(g, t - mixing_at[g])
        steps += sorted(tick, key=lambda st: ORDER.get(st[0], ORDER["others"]))
    return steps


def build(nc, x, ctxT, mask, pack, wkv96, br, w1, w2, out):
    steps = plan()
    nth = {}
    seen = {}
    for st in steps:
        seen[st[0]] = seen.get(st[0], 0) + 1
        nth[st] = seen[st[0]]
    SHARED = ("turn", "key", "value", "receptance", "mixed", "query", "context", "probs_v",
              "turn_heads", "attended", "router", "gated")
    shared = {st: i for i, st in enumerate(s for s in steps if s[0] in SHARED)}

    with ExitStack() as ctx:
        def sb(name, shape, dt=F32):
            return ctx.enter_context(nc.sbuf_tensor(name, shape, dt))

        def ps(name):
            return ctx.enter_context(nc.psum_tensor(name, [P, 512], F32))

        def sem(name):
            return ctx.enter_context(nc.semaphore(name))

        resid = sb("resid", [P, B, C])
        pk = sb("pk", [P, PACKED])
        w96 = sb("w96", [CTX, 2 * C])
        ctx_sb = sb("ctx_sb", [CTX, B, M])
        br_sb = sb("br_sb", [1, E])
        w1_raw = sb("w1_raw", [P, RAW, F])
        w1_hi = sb("w1_hi", [P, E * F], F32R)
        w1_lo = sb("w1_lo", [P, E * F], F32R)
        w2_sb = sb("w2_sb", [P, NS * C])
        mask_u8 = sb("mask_u8", [P, B * M], U8)
        mask_bias = sb("mask_bias", [P, B, M], BF16)
        ones_b = sb("ones_b", [P, P], BF16)
        ones_f = sb("ones_f", [1, P])
        half_neg = sb("half_neg", [P, GB])
        mix_c = sb("mix_c", [P, 3])
        w_now = sb("w_now", [P, 3, C])
        w_before = sb("w_before", [P, 3, C])
        decay_w = sb("decay_w", [P, 1])
        decay_row = sb("decay_row", [P, NPAD])
        bn = sb("bn", [P, B, 6])
        mv = sb("mv", [P, 3, B, 2])
        var_e = sb("var_e", [P, 3, B])
        rstd = sb("rstd", [P, 3, B])
        xn = sb("xn", [P, B, C])
        xT1 = sb("xT1", [P, 2, NPAD])
        xT2 = sb("xT2", [P, N])
        xT3 = sb("xT3", [P, N])
        x_hi = sb("x_hi", [P, 2, N], F32R)
        x_lo = sb("x_lo", [P, 2, N], F32R)
        k_sb = sb("k_sb", [P, NPAD])
        v_sb = sb("v_sb", [P, NPAD])
        er = sb("er", [P, N])
        mx = sb("mx", [P, NPAD])
        ex = sb("ex", [P, 4, NPAD])
        ev = sb("ev", [P, NPAD])
        num = sb("num", [P, NPAD])
        den = sb("den", [P, NPAD])
        ta = sb("ta", [P, N])
        tb = sb("tb", [P, N])
        tc = sb("tc", [P, N])
        rwkv = sb("rwkv", [P, N])
        qT = sb("qT", [P, 2, N])
        ctx4 = sb("ctx4", [CTX, CTX_RING, SP])
        kbd = sb("kbd", [P, 3, SQ])
        vbd = sb("vbd", [P, 3, KT * H * (HD + 1)])
        smax = sb("smax", [P, 2, QH])
        prob = sb("prob", [P, PROBS, SP])
        probT = sb("probT", [P, 3, SP])
        rsum = sb("rsum", [P, 2, QH])
        heads = sb("heads", [P, 2, C])
        headsT = sb("headsT", [P, 2, C])
        xs = sb("xs", [P, GB, E])
        diff = sb("diff", [P, GB, E])
        above = sb("above", [P, GB, 2, E])
        top = sb("top", [P, GB])
        tau = sb("tau", [P, GB])
        sums = sb("sums", [P, GB, 2])
        inv = sb("inv", [P, GB])
        gates = sb("gates", [P, 2, GB, E])
        hid = sb("hid", [P, 4, N])
        yT = sb("yT", [P, 2, N])

        bank_z = [ps("bank_z0"), ps("bank_z1")]
        bank_y = ps("bank_y")
        bank_s = [ps("bank_s0"), ps("bank_s1")]
        bank_p = ps("bank_p")
        bank_m = [ps("bank_m0"), ps("bank_m1")]

        x_in = [sem(f"x_in{g}") for g in range(G)]
        pack_in, ctx_in, small_in = sem("pack_in"), sem("ctx_in"), sem("small_in")
        w1_in, w2_in = [sem(f"w1_in{e}") for e in range(E)], sem("w2_in")
        w1_hi_ready, w1_split = sem("w1_hi_ready"), sem("w1_split")
        pool_step = sem("pool_step")
        pool_const, dve_const, act_const = sem("pool_const"), sem("dve_const"), sem("act_const")
        dve_step = sem("dve_step")
        stats_ready, rstd_ready, normed = sem("stats_ready"), sem("rstd_ready"), sem("normed")
        full = [sem("full0"), sem("full1")]
        freed = [sem("freed0"), sem("freed1")]
        er_ready = sem("er_ready")
        exponents_ready, exps_ready, rwkv_ready = sem("exponents_ready"), sem("exps_ready"), sem("rwkv_ready")
        maximum_ready, exponent1_ready = sem("maximum_ready"), sem("exponent1_ready")
        den_ready, denominator_ready = sem("den_ready"), sem("denominator_ready")
        inverted = sem("inverted")
        mixing_read = sem("mixing_read")
        ctx4_ready, context_ready = sem("ctx4_ready"), sem("context_ready")
        scores_full, scores_read = sem("scores_full"), sem("scores_read")
        exp_ready, probs_turned, probT_ready = sem("exp_ready"), sem("probs_turned"), sem("probT_ready")
        heads_ready = sem("heads_ready")
        gates_ready = sem("gates_ready")
        hi_ready, lo_ready = sem("hi_ready"), sem("lo_ready")
        z_full, hid_ready, hid_used = sem("z_full"), sem("hid_ready"), sem("hid_used")
        y_full, y_ready = sem("y_full"), sem("y_ready")
        stored = sem("stored")

        def part(name):
            return pk[:, PACK[name][0]:PACK[name][1]]

        ident = part("ident")
        cols = part("cols")
        first = cols[:, 1:2]

        def now(t):
            return t.rearrange("p (b t) -> p b t", t=TP)[:, :, 1:TP]

        def before(t):
            return t.rearrange("p (b t) -> p b t", t=TP)[:, :, 0:T]

        def pads(t):
            return t.rearrange("p (b t) -> p b t", t=TP)[:, :, 0:1]

        def by_batch(t):
            return t.rearrange("p (b t) -> p b t", t=T)

        def tok(g):
            return SIZES[g] * T

        def npad(g):
            return SIZES[g] * TP

        def shared_bank(st):
            return bank_m[shared[st] % 2]

        def wait_full(eng, st):
            eng.wait_ge(full[shared[st] % 2], shared[st] // 2 + 1)

        def wait_moved(eng, st):
            eng.wait_ge(freed[shared[st] % 2], shared[st] // 2 + 1)

        def wait_bank(eng, st):
            if shared[st] >= 2:
                eng.wait_ge(freed[shared[st] % 2], shared[st] // 2)

        def fill_done(ins, st):
            ins.then_inc(full[shared[st] % 2], 1)

        def moved(ins, st):
            ins.then_inc(freed[shared[st] % 2], 1)

        def wait_down(eng, i):
            if i % FT == FT - 1:
                eng.wait_ge(y_full, i // FT + 1)
            else:
                eng.wait_ge(hid_used, i // FT * (FT - 1) + i % FT + 1)

        def batches(g, b):
            return range(START[g], START[g] + SIZES[g]) if b is None else range(START[g] + b, START[g] + b + 1)

        def group_of(i):
            g = max(g for g in range(G) if START[g] <= i)
            return g, i - START[g]

        def unit(n):
            g, b = group_of(n // NQ)
            return g, NQ * b + n % NQ

        block = ctx.enter_context(nc.Block())

        @block.sync
        def _(sp):
            sp.dma_start(resid[:, 0:SIZES[0], :], x[:, 0:SIZES[0], :]).then_inc(x_in[0], 16)
            sp.dma_start(pk[:, :], pack).then_inc(pack_in, 16)
            sp.dma_start(w96[:, :], wkv96).then_inc(ctx_in, 16)
            sp.dma_start(ctx_sb[:, :, :], ctxT).then_inc(ctx_in, 16)
            sp.dma_start(br_sb[:, :], br).then_inc(small_in, 16)
            sp.dma_start(mask_u8[:, :], mask.broadcast_to([P, B * M])).then_inc(small_in, 16)
            for g in range(1, G):
                at = slice(START[g], START[g] + SIZES[g])
                sp.dma_start(resid[:, at, :], x[:, at, :]).then_inc(x_in[g], 16)
            for e in range(E):
                if e >= RAW:
                    sp.wait_ge(w1_split, e - RAW + 1)
                sp.dma_start(w1_raw[:, e % RAW, :], w1[:, e * F:(e + 1) * F]).then_inc(w1_in[e], 16)
                if e == 1:
                    sp.dma_start(w2_sb[:, :], w2).then_inc(w2_in, 16)
            for g in range(G):
                wait_moved(sp, ("gated", g, E - 1))
                at = slice(START[g], START[g] + SIZES[g])
                sp.dma_start(out[:, at, :], resid[:, at, :]).then_inc(stored, 16)
            sp.wait_ge(stored, 16 * G)

        @block.gpsimd
        def _(pool):
            chain = [0]

            def link(ins):
                chain[0] += 1
                ins.then_inc(pool_step, 1)
                pool.wait_ge(pool_step, chain[0])

            nc.gpsimd.memset(half_neg[:, :], -0.5)
            nc.gpsimd.memset(ctx4[:, :, SQ:SP], 0.0)
            nc.gpsimd.memset(ones_b[:, :], 1.0)
            nc.gpsimd.memset(ones_f[:, :], 1.0)
            nc.gpsimd.memset(prob[:, :, SQ:SP], 0.0)
            for t, value in ((xT1[:, 0, :], 0.0), (xT1[:, 1, :], 0.0), (ex[:, 0, :], 0.0), (ex[:, 1, :], 0.0),
                             (ev[:, :], 0.0), (k_sb[:, :], NEG)):
                ins = nc.gpsimd.memset(pads(t), value)
            ins.then_inc(pool_const, 1)
            pool.wait_ge(pool_const, 1)

            def split_w1(e):
                pool.wait_ge(w1_hi_ready, e + 1)
                hi, raw = w1_hi[:, e * F:(e + 1) * F], w1_raw[:, e % RAW, :]
                nc.gpsimd.tensor_tensor(w1_lo[:, e * F:(e + 1) * F], raw, hi.bitcast(F32), ALU.subtract)\
                    .then_inc(w1_split, 1)

            def stats(st):
                _, k, g, b = st
                pool.wait_ge(stats_ready, nth[st])
                at = batches(g, b)
                lo, hi = at[0], at[-1] + 1
                v = var_e[:, k, lo:hi]
                link(nc.gpsimd.tensor_scalar(v, mv[:, k, lo:hi, 1], EPS, 1.0, ALU.add, ALU.mult))
                nc.gpsimd.tensor_tensor(rstd[:, k, lo:hi], v, half_neg[:, 0:hi - lo], ALU.pow)\
                    .then_inc(rstd_ready, 1)

            def replicate(i):
                if i == 0:
                    pool.wait_ge(ctx_in, 32)
                if i >= CTX_RING:
                    wait_full(pool, ("context", *group_of(i - CTX_RING)))
                nc.gpsimd.tensor_copy(ctx4[:, i % CTX_RING, 0:SQ].rearrange("p (h m) -> p h m", m=M),
                                      ctx_sb[:, i:i + 1, :].broadcast_to([CTX, QH, M]))\
                    .then_inc(ctx4_ready, 1)

            def exponent1(g):
                n = npad(g)
                pool.wait_ge(maximum_ready, g + 1)
                nc.gpsimd.tensor_tensor(now(ex[:, 1, 0:n]), now(k_sb[:, 0:n]), now(mx[:, 0:n]), ALU.subtract)\
                    .then_inc(exponent1_ready, 1)

            def denominator(g):
                n, m = npad(g), tok(g)
                b, c = by_batch(tb[:, 0:m]), by_batch(tc[:, 0:m])
                e1, e2 = now(ex[:, 2, 0:n]), now(ex[:, 3, 0:n])
                if g >= 1:
                    pool.wait_ge(rwkv_ready, g)
                wait_moved(pool, ("value", g))
                pool.wait_ge(exps_ready, 4 * g + 4)
                nc.gpsimd.tensor_tensor(b, e2, now(v_sb[:, 0:n]), ALU.mult)
                pool.wait_ge(den_ready, g + 1)
                link(nc.gpsimd.tensor_tensor(c, e1, before(den[:, 0:n]), ALU.mult))
                nc.gpsimd.tensor_tensor(c, c, e2, ALU.add).then_inc(denominator_ready, 1)

            for st in steps:
                if st[0] == "exponent" and st[2] == 1:
                    exponent1(st[1])
                if st[0] == "denominator":
                    denominator(st[1])
                if st[0] == "stats":
                    stats(st)
                if st[0] == "stats" and st[1] == 0 and st[2] == 0:
                    for i in range(CTX_RING):
                        replicate(i)
                if st[0] == "context" and START[st[1]] + st[2] + CTX_RING < B:
                    replicate(START[st[1]] + st[2] + CTX_RING)
                if st[0] == "split":
                    split_w1(st[1])

        @block.scalar
        def _(act):
            act.wait_ge(pack_in, 16)
            nc.scalar.activation(decay_w[:, :], cols[:, 0:1], ACT.Exp).then_inc(act_const, 1)
            act.wait_ge(pool_const, 1)

            def split(st):
                e = st[1]
                act.wait_ge(w1_in[e], 16)
                nc.scalar.activation(w1_hi[:, e * F:(e + 1) * F], w1_raw[:, e % RAW, :], ACT.Copy)\
                    .then_inc(w1_hi_ready, 1)

            def turn(st):
                _, k, g, b = st
                wait_full(act, st)
                src = shared_bank(st)
                if k == 0:
                    if g >= 2:
                        wait_full(act, ("receptance", g - 2))
                    moved(nc.scalar.activation(now(xT1[:, g % 2, 0:npad(g)]), by_batch(src[:, 0:tok(g)]), ACT.Copy),
                          st)
                elif k == 1:
                    if g >= 1:
                        wait_full(act, ("query", g - 1))
                    moved(nc.scalar.activation(xT2[:, 0:tok(g)], src[:, 0:tok(g)], ACT.Copy), st)
                else:
                    at = slice(b * T, b * T + T)
                    if g >= 1:
                        wait_full(act, ("router", g - 1))
                    if g >= 2:
                        act.wait_ge(z_full, NS * (g - 1))
                    nc.scalar.activation(x_hi[:, g % 2, at], src[:, 0:T], ACT.Copy).then_inc(hi_ready, 1)
                    moved(nc.scalar.activation(xT3[:, at], src[:, 0:T], ACT.Copy), st)

            def key(st):
                g = st[1]
                wait_full(act, st)
                if g >= 1:
                    act.wait_ge(mixing_read, g)
                moved(nc.scalar.activation(now(k_sb[:, 0:npad(g)]), by_batch(shared_bank(st)[:, 0:tok(g)]), ACT.Copy), st)

            def value(st):
                g = st[1]
                wait_full(act, st)
                moved(nc.scalar.activation(now(v_sb[:, 0:npad(g)]), by_batch(shared_bank(st)[:, 0:tok(g)]), ACT.Copy), st)

            def receptance(st):
                wait_full(act, st)
                n = tok(st[1])
                moved(nc.scalar.activation(er[:, 0:n], shared_bank(st)[:, 0:n], ACT.Exp, scale=-1.0), st)

            def exp(st):
                _, g, i = st
                if i == 1:
                    act.wait_ge(exponent1_ready, g + 1)
                else:
                    act.wait_ge(exponents_ready, 2 * g + min(i, 2) // 2 + 1)
                e = now(ex[:, i, 0:npad(g)])
                nc.scalar.activation(e, e, ACT.Exp).then_inc(exps_ready, 1)

            def query(st):
                g = st[1]
                wait_full(act, st)
                if g >= 2:
                    act.wait_ge(scores_full, NQ * START[g - 1])
                n = tok(g)
                moved(nc.scalar.activation(qT[:, g % 2, 0:n], shared_bank(st)[:, 0:n], ACT.Copy), st)

            def scores(st):
                u = nth[st] - 1
                act.wait_ge(scores_read, u + 1)
                pr = prob[:, u % PROBS, 0:SQ]
                nc.scalar.activation(pr, pr, ACT.Exp).then_inc(exp_ready, 1)

            def turn_probs(st):
                u = nth[st] - 1
                act.wait_ge(probs_turned, u + 1)
                if u >= 3:
                    wait_full(act, ("probs_v", *unit(u - 3)))
                nc.scalar.activation(probT[:, u % 3, :], bank_p[:, 0:SP], ACT.Copy).then_inc(probT_ready, 1)

            def turn_heads(st):
                i = nth[st] - 1
                wait_full(act, st)
                if i >= 2:
                    wait_full(act, ("attended", *group_of(i - 2)))
                moved(nc.scalar.activation(headsT[:, i % 2, :], shared_bank(st)[:, 0:C], ACT.Copy), st)

            def router(st):
                g = st[1]
                wait_full(act, st)
                if g >= 1:
                    act.wait_ge(gates_ready, g)
                n = SIZES[g]
                moved(nc.scalar.activation(xs[:, 0:n, :], shared_bank(st)[:, 0:n * E]
                                           .rearrange("p (b e) -> p b e", e=E), ACT.Copy, scale=0.5), st)

            def hidden(st):
                i, s, n = nth[st] - 1, st[2], tok(st[1])
                act.wait_ge(z_full, i + 1)
                if i >= 4:
                    wait_down(act, i - 4)
                nc.scalar.activation(hid[:, i % 4, 0:n], bank_z[i % 2][:, 0:n], ACT.Relu,
                                     bias=part("b1")[:, s:s + 1]).then_inc(hid_ready, 1)

            def down(st):
                _, g, s = st
                if s % FT < FT - 1:
                    return
                e = s // FT
                i = E * g + e
                act.wait_ge(y_full, i + 1)
                if i >= 2:
                    wait_full(act, ("gated", (i - 2) // E, (i - 2) % E))
                n = tok(g)
                nc.scalar.activation(yT[:, i % 2, 0:n], bank_y[:, 0:n], ACT.Identity,
                                     bias=part("b2")[:, e:e + 1]).then_inc(y_ready, 1)

            run = {"split": split, "turn": turn, "key": key, "value": value, "receptance": receptance, "exp": exp,
                   "query": query, "scores": scores, "turn_probs": turn_probs, "turn_heads": turn_heads,
                   "router": router, "hidden": hidden, "down": down}
            for st in steps:
                if st[0] in run:
                    run[st[0]](st)

        @block.vector
        def _(dve):
            chain = [0]

            def link(ins):
                chain[0] += 1
                ins.then_inc(dve_step, 1)
                dve.wait_ge(dve_step, chain[0])

            v = nc.vector

            def weights():
                v.memset(decay_row[:, :], 0.0).then_inc(dve_step, 1)
                chain[0] += 1
                dve.wait_ge(pack_in, 16)
                dve.wait_ge(pool_const, 1)
                link(v.tensor_scalar(mix_c[:, :], cols[:, 2:5], -1.0, 1.0, ALU.mult, ALU.add))
                for i, name in enumerate(("wkT", "wvT", "wrT")):
                    v.tensor_scalar(w_now[:, i, :], part(name), cols[:, 2 + i:3 + i], None, ALU.mult)
                    ins = v.tensor_scalar(w_before[:, i, :], part(name), mix_c[:, i:i + 1], None, ALU.mult)
                ins.then_inc(dve_const, 1)
                dve.wait_ge(act_const, 1)
                v.tensor_scalar(now(decay_row[:, :]), now(decay_row[:, :]), decay_w[:, 0:1], None, ALU.subtract)\
                    .then_inc(dve_step, 1)
                v.memset(pads(decay_row[:, :]), NEG).then_inc(dve_step, 1)
                chain[0] += 2

            def consts():
                dve.wait_ge(small_in, 32)
                v.tensor_scalar(mask_bias[:, :, :].rearrange("p b m -> p (b m)"), mask_u8[:, :],
                                -1.0, MASKED, ALU.add, ALU.mult).then_inc(dve_const, 1)
                for i in range(3):
                    v.tensor_copy(vbd[:, i, :].rearrange("p (k d) -> p k d", d=HD + 1)[:, :, HD], part("vmask"))

            def stats(st):
                _, k, g, b = st
                if k == 0:
                    dve.wait_ge(x_in[g], 16)
                for i in batches(g, b):
                    ins = v.bn_stats(bn[:, i, :], resid[:, i, :])
                link(ins)
                for i in batches(g, b):
                    ins = v.bn_aggr(mv[:, k, i, :], bn[:, i, :])
                ins.then_inc(stats_ready, 1)
                if (k, g) == (0, 0):
                    weights()

            def norm(st):
                _, k, g, b = st
                dve.wait_ge(rstd_ready, nth[("stats", k, g, b if k == 2 else None)])
                i = START[g] + b
                v.tensor_scalar(xn[:, i, :], resid[:, i, :], mv[:, k, i, 0:1], rstd[:, k, i:i + 1],
                                ALU.subtract, ALU.mult).then_inc(normed, 1)

            def turn(st):
                _, k, g, b = st
                if k == 2:
                    wait_moved(dve, st)
                    if g >= 2:
                        dve.wait_ge(z_full, NS * (g - 1))
                    at = slice(b * T, b * T + T)
                    v.tensor_tensor(x_lo[:, g % 2, at], xT3[:, at], x_hi[:, g % 2, at].bitcast(F32),
                                    ALU.subtract).then_inc(lo_ready, 1)

            def maximum(st):
                g = st[1]
                n = npad(g)
                wait_moved(dve, ("key", g))
                if g == 0:
                    dve.wait_ge(dve_step, chain[0])
                v.tensor_tensor_scan(mx[:, 0:n], decay_row[:, 0:n], k_sb[:, 0:n], NEG, ALU.add, ALU.max)\
                    .then_inc(maximum_ready, 1)
                dve.wait_ge(maximum_ready, g + 1)

            def exponent(st):
                _, g, i = st
                n = npad(g)
                old, new = before(mx[:, 0:n]), now(mx[:, 0:n])
                e, a = now(ex[:, i, 0:n]), by_batch(ta[:, 0:tok(g)])
                if i == 0:
                    v.scalar_tensor_tensor(e, old, decay_w[:, 0:1], new, ALU.subtract, ALU.subtract)\
                        .then_inc(exponents_ready, 1)
                elif i == 2:
                    link(v.scalar_tensor_tensor(a, now(k_sb[:, 0:n]), first, old, ALU.add, ALU.subtract))
                elif i == 3:
                    v.tensor_scalar(now(ex[:, 2, 0:n]), a, -1.0, 0.0, ALU.mult, ALU.min)
                    v.tensor_scalar(e, a, 0.0, None, ALU.min).then_inc(exponents_ready, 1)

            def weighted(st):
                g = st[1]
                n = npad(g)
                dve.wait_ge(exps_ready, 4 * g + 2)
                wait_moved(dve, ("value", g))
                link(v.tensor_tensor(now(ev[:, 0:n]), now(ex[:, 1, 0:n]), now(v_sb[:, 0:n]), ALU.mult))

            def scan_den(st):
                n = npad(st[1])
                v.tensor_tensor_scan(den[:, 0:n], ex[:, 0, 0:n], ex[:, 1, 0:n], 0.0, ALU.mult, ALU.add)\
                    .then_inc(den_ready, 1)

            def scan_num(st):
                n = npad(st[1])
                link(v.tensor_tensor_scan(num[:, 0:n], ex[:, 0, 0:n], ev[:, 0:n], 0.0, ALU.mult, ALU.add))

            def numerator(st):
                _, g, i = st
                n, m = npad(g), tok(g)
                a = by_batch(ta[:, 0:m])
                if i == 0:
                    dve.wait_ge(exps_ready, 4 * g + 3)
                    link(v.tensor_tensor(a, now(ex[:, 2, 0:n]), before(num[:, 0:n]), ALU.mult))
                else:
                    dve.wait_ge(denominator_ready, g + 1)
                    link(v.tensor_tensor(a, a, by_batch(tb[:, 0:m]), ALU.add))

            def receive(st):
                g = st[1]
                m = tok(g)
                wait_moved(dve, ("receptance", g))
                v.scalar_tensor_tensor(tb[:, 0:m], er[:, 0:m], 1.0, tc[:, 0:m], ALU.add, ALU.mult)\
                    .then_inc(mixing_read, 1)

            def inverse(st):
                _, g, i = st
                m = tok(g)
                dve.wait_ge(mixing_read, g + 1)
                at = slice(i * m // 4, (i + 1) * m // 4)
                v.reciprocal(tc[:, at], tb[:, at]).then_inc(inverted, 1)

            def rwkv_(st):
                g = st[1]
                m = tok(g)
                if g >= 1:
                    wait_full(dve, ("mixed", g - 1))
                dve.wait_ge(inverted, 4 * (g + 1))
                v.tensor_tensor(rwkv[:, 0:m], ta[:, 0:m], tc[:, 0:m], ALU.mult).then_inc(rwkv_ready, 1)

            def mixed(st):
                g = st[1]
                wait_full(dve, st)
                r = resid[:, START[g]:START[g] + SIZES[g], :]
                moved(v.tensor_tensor(r, r, by_batch(shared_bank(st)[:, 0:tok(g)]), ALU.add), st)
                wait_moved(dve, st)

            def context(st):
                i = nth[st] - 1
                if i == 0:
                    consts()
                wait_full(dve, st)
                if i >= 3:
                    wait_full(dve, ("probs_v", *unit(NQ * (i - 3) + NQ - 1)))
                src = shared_bank(st)
                v.tensor_tensor(kbd[:, i % 3, :].rearrange("p (h m) -> p h m", m=M),
                                src[:, 0:M].rearrange("p (o m) -> p o m", o=1).broadcast_to([P, QH, M]),
                                part("qmask").rearrange("p (h o) -> p h o", o=1).broadcast_to([P, QH, M]),
                                ALU.mult).then_inc(context_ready, 1)
                moved(v.tensor_tensor(
                    vbd[:, i % 3, :].rearrange("p (k d) -> p k d", d=HD + 1)[:, :, 0:HD],
                    src[:, P:P + KT * C].rearrange("p (k d) -> p k d", d=HD),
                    part("vmask").rearrange("p (k o) -> p k o", o=1).broadcast_to([P, KT * H, HD]),
                    ALU.mult), st)

            def scores(st):
                u = nth[st] - 1
                dve.wait_ge(scores_full, u + 1)
                s = bank_s[u % 2][:, 0:SQ].rearrange("p (h m) -> p h m", m=M)
                link(v.tensor_reduce(smax[:, u % 2, :], s, AX_X, ALU.max))
                if u >= PROBS:
                    dve.wait_ge(probs_turned, u - PROBS + 1)
                v.tensor_tensor(prob[:, u % PROBS, 0:SQ].rearrange("p (h m) -> p h m", m=M), s,
                                smax[:, u % 2, :].rearrange("p (h o) -> p h o", o=1).broadcast_to([P, QH, M]),
                                ALU.subtract).then_inc(scores_read, 1)

            def probs_v(st):
                _, g, u = st
                wait_full(dve, st)
                o = shared_bank(st)[:, 0:QH * (HD + 1)].rearrange("p (h d) -> p h d", d=HD + 1)
                i = START[g] + u // NQ
                rs = rsum[:, u % 2, :].rearrange("p (h o) -> p h o", o=1)
                link(v.reciprocal(rs, o[:, :, HD:HD + 1]))
                if u % NQ == 0 and i >= 2:
                    wait_full(dve, ("turn_heads", *group_of(i - 2)))
                q = u % NQ
                moved(v.tensor_tensor(heads[:, i % 2, q * QH * HD:(q + 1) * QH * HD]
                                      .rearrange("p (h d) -> p h d", d=HD),
                                      o[:, :, 0:HD], rs.broadcast_to([P, QH, HD]), ALU.mult), st)

            def attended(st):
                _, g, b = st
                wait_full(dve, st)
                r = resid[:, START[g] + b, :]
                moved(v.tensor_tensor(r, r, shared_bank(st)[:, 0:C], ALU.add), st)
                wait_moved(dve, st)

            def wide(t, n):
                return t.rearrange("p (b o) -> p b o", o=1).broadcast_to([P, n, E])

            def router(st):
                g = st[1]
                n = SIZES[g]
                wait_moved(dve, st)
                link(v.tensor_reduce(top[:, 0:n], xs[:, 0:n, :], AX_X, ALU.max))
                v.tensor_tensor(xs[:, 0:n, :], xs[:, 0:n, :], wide(top[:, 0:n], n), ALU.subtract)
                link(v.memset(tau[:, 0:n], -1.0))

            def threshold(st):
                _, g, i = st
                n = SIZES[g]
                d, a, a2 = diff[:, 0:n, :], above[:, 0:n, 0, :], above[:, 0:n, 1, :]
                t, s1, s2, iv = tau[:, 0:n], sums[:, 0:n, 0], sums[:, 0:n, 1], inv[:, 0:n]
                link(v.tensor_tensor(d, xs[:, 0:n, :], wide(t, n), ALU.subtract))
                v.tensor_scalar(a, d, 0.0, None, ALU.max)
                link(v.scalar_tensor_tensor(a2, d, 0.0, d, ALU.max, ALU.mult))
                link(v.tensor_reduce(sums[:, 0:n, :], above[:, 0:n, :, :], AX_X, ALU.add))
                if i < NEWTON:
                    link(v.reciprocal(iv, s1))
                    link(v.scalar_tensor_tensor(iv, s2, -1.0, iv, ALU.add, ALU.mult))
                    link(v.scalar_tensor_tensor(t, iv, 0.5, t, ALU.mult, ALU.add))
                else:
                    link(v.reciprocal(iv, s2))
                    link(v.tensor_tensor(a, a2, wide(iv, n), ALU.mult))
                    v.scalar_tensor_tensor(gates[:, g % 2, 0:n, :], a, THRESH, a, ALU.is_gt, ALU.mult)\
                        .then_inc(gates_ready, 1)

            def gated(st):
                _, g, e = st
                if e == 0:
                    dve.wait_ge(gates_ready, g + 1)
                wait_full(dve, st)
                if e > 0:
                    wait_moved(dve, ("gated", g, e - 1))
                src = shared_bank(st)
                for b in range(SIZES[g]):
                    r = resid[:, START[g] + b, :]
                    ins = v.scalar_tensor_tensor(r, src[:, b * C:(b + 1) * C], gates[:, g % 2, b, e:e + 1], r,
                                                 ALU.mult, ALU.add)
                moved(ins, st)

            run = {"stats": stats, "norm": norm, "turn": turn, "maximum": maximum,
                   "exponent": exponent, "weighted": weighted, "scan_den": scan_den, "scan_num": scan_num,
                   "numerator": numerator, "receive": receive, "inverse": inverse, "rwkv": rwkv_,
                   "threshold": threshold, "mixed": mixed, "context": context, "scores": scores, "probs_v": probs_v,
                   "attended": attended, "router": router, "gated": gated}
            for st in steps:
                if st[0] in run:
                    run[st[0]](st)

        @block.tensor
        def _(pe):
            mm = nc.tensor.matmul
            pe.wait_ge(pack_in, 16)
            pe.wait_ge(dve_const, 1)
            pe.wait_ge(pool_const, 1)

            def turn(st):
                _, k, g, b = st
                pe.wait_ge(normed, nth[("norm", k, g, SIZES[g] - 1 if b is None else b)])
                wait_bank(pe, st)
                for n, i in enumerate(batches(g, b)):
                    ins = nc.tensor.transpose(shared_bank(st)[:, n * T:(n + 1) * T], xn[:, i, :], ident)
                fill_done(ins, st)

            def project(st, i):
                g = st[1]
                wait_moved(pe, ("turn", 0, g, None))
                wait_bank(pe, st)
                dst, src = by_batch(shared_bank(st)[:, 0:tok(g)]), xT1[:, g % 2, 0:npad(g)]
                mm(dst, w_now[:, i, :], now(src), start=True, stop=False)
                fill_done(mm(dst, w_before[:, i, :], before(src), start=False, stop=True), st)

            def mixed(st):
                g = st[1]
                pe.wait_ge(rwkv_ready, g + 1)
                wait_bank(pe, st)
                for b in range(SIZES[g]):
                    ins = mm(shared_bank(st)[:, b * C:(b + 1) * C], rwkv[:, b * T:(b + 1) * T], part("woT"),
                             start=True, stop=True)
                fill_done(ins, st)

            def query(st):
                wait_moved(pe, ("turn", 1, st[1], None))
                wait_bank(pe, st)
                n = tok(st[1])
                fill_done(mm(shared_bank(st)[:, 0:n], part("Wq"), xT2[:, 0:n], start=True, stop=True), st)

            def context(st):
                i = nth[st] - 1
                if i == 0:
                    pe.wait_ge(ctx_in, 32)
                pe.wait_ge(ctx4_ready, i + 1)
                wait_bank(pe, st)
                dst = shared_bank(st)
                mm(dst[:, 0:M], w96[:, 0:C], ctx_sb[:, i, :], start=True, stop=True)
                for k in range(KT):
                    ins = mm(dst[:, P + k * C:P + (k + 1) * C], ctx4[:, i % CTX_RING, k * P:(k + 1) * P],
                             w96[:, C:2 * C], start=True, stop=True)
                fill_done(ins, st)

            def scores(st):
                _, g, u = st
                if u % 2:
                    return
                b, q = u // NQ, u % NQ
                i = START[g] + b
                n = nth[st] - 1
                if u == 0:
                    wait_moved(pe, ("query", g))
                if q == 0:
                    pe.wait_ge(context_ready, i + 1)
                if n == 0:
                    pe.wait_ge(dve_const, 2)
                if n >= 2:
                    pe.wait_ge(scores_read, n)
                for j in range(2):
                    rows = slice(32 * (q + j), 32 * (q + j) + 32)
                    mm(bank_s[j][:, 0:SQ], qT[rows, g % 2, b * T:(b + 1) * T], kbd[rows, i % 3, :],
                       start=True, stop=False)
                for j in range(2):
                    row = slice(32 * (q + j), 32 * (q + j) + 1)
                    mm(bank_s[j][:, 0:SQ].rearrange("p (h m) -> p h m", m=M), ones_b[row, :],
                       mask_bias[row, i:i + 1, :].broadcast_to([1, QH, M]),
                       start=False, stop=True).then_inc(scores_full, 1)

            def turn_probs(st):
                n = nth[st] - 1
                pe.wait_ge(exp_ready, n + 1)
                if n >= 1:
                    pe.wait_ge(probT_ready, n)
                for k in range(KT):
                    ins = nc.tensor.transpose(bank_p[:, k * P:(k + 1) * P], prob[:, n % PROBS, k * P:(k + 1) * P],
                                              ident)
                ins.then_inc(probs_turned, 1)

            def probs_v(st):
                _, g, u = st
                n = nth[st] - 1
                i, q = n // NQ, n % NQ
                pe.wait_ge(probT_ready, n + 1)
                if q == 0:
                    wait_moved(pe, ("context", g, u // NQ))
                wait_bank(pe, st)
                w = QH * (HD + 1)
                for k in range(KT):
                    at = (k * H + q * QH) * (HD + 1)
                    ins = mm(shared_bank(st)[:, 0:w], probT[:, n % 3, k * P:(k + 1) * P],
                             vbd[:, i % 3, at:at + w], start=(k == 0), stop=(k == KT - 1))
                fill_done(ins, st)

            def turn_heads(st):
                _, g, b = st
                i = nth[st] - 1
                wait_moved(pe, ("probs_v", g, NQ * b + NQ - 1))
                wait_moved(pe, ("probs_v", g, NQ * b + NQ - 2))
                wait_bank(pe, st)
                fill_done(nc.tensor.transpose(shared_bank(st)[:, 0:T], heads[:, i % 2, :], ident), st)

            def attended(st):
                i = nth[st] - 1
                wait_moved(pe, ("turn_heads", st[1], st[2]))
                wait_bank(pe, st)
                fill_done(mm(shared_bank(st)[:, 0:C], headsT[:, i % 2, :], part("Wo"), start=True, stop=True), st)

            def router(st):
                g = st[1]
                for b in range(SIZES[g]):
                    wait_moved(pe, ("turn", 2, g, b))
                wait_bank(pe, st)
                for b in range(SIZES[g]):
                    dst = shared_bank(st)[:, b * E:(b + 1) * E]
                    mm(dst, xT3[:, b * T:(b + 1) * T], part("Wr"), start=True, stop=False)
                    ins = mm(dst, ones_f[0:1, :], br_sb[0:1, :], start=False, stop=True)
                fill_done(ins, st)

            def hidden(st):
                _, g, s = st
                n = nth[st] - 1
                if s == 0:
                    pe.wait_ge(hi_ready, START[g] + SIZES[g])
                    pe.wait_ge(lo_ready, START[g] + SIZES[g])
                if g == 0 and s % FT == 0:
                    pe.wait_ge(w1_split, s // FT + 1)
                if n >= 2:
                    pe.wait_ge(hid_ready, n - 1)
                at = slice(s * P, (s + 1) * P)
                z, hi, lo = bank_z[n % 2][:, 0:tok(g)], x_hi[:, g % 2, 0:tok(g)], x_lo[:, g % 2, 0:tok(g)]
                mm(z, w1_lo[:, at], hi, start=True, stop=False)
                mm(z, w1_hi[:, at], lo, start=False, stop=False)
                mm(z, w1_hi[:, at], hi, start=False, stop=True).then_inc(z_full, 1)

            def down(st):
                _, g, s = st
                n = nth[st] - 1
                if n == 0:
                    pe.wait_ge(w2_in, 16)
                pe.wait_ge(hid_ready, n + 1)
                if s % FT == 0 and n > 0:
                    pe.wait_ge(y_ready, n // FT)
                ins = mm(bank_y[:, 0:tok(g)], w2_sb[:, s * C:(s + 1) * C], hid[:, n % 4, 0:tok(g)],
                         start=(s % FT == 0), stop=(s % FT == FT - 1))
                if s % FT == FT - 1:
                    ins.then_inc(y_full, 1)
                else:
                    ins.then_inc(hid_used, 1)

            def gated(st):
                n = nth[st] - 1
                pe.wait_ge(y_ready, n + 1)
                wait_bank(pe, st)
                for b in range(SIZES[st[1]]):
                    ins = nc.tensor.transpose(shared_bank(st)[:, b * C:(b + 1) * C],
                                              yT[:, n % 2, b * T:(b + 1) * T], ident)
                fill_done(ins, st)

            run = {"turn": turn, "key": lambda st: project(st, 0), "value": lambda st: project(st, 1),
                   "receptance": lambda st: project(st, 2), "mixed": mixed, "query": query,
                   "context": context, "scores": scores, "turn_probs": turn_probs, "probs_v": probs_v,
                   "turn_heads": turn_heads, "attended": attended, "router": router, "hidden": hidden,
                   "down": down, "gated": gated}
            for st in steps:
                if st[0] in run:
                    run[st[0]](st)


def kernel(x, ctx_768, mask_BxS2_bf1, L0_attn_wk, L0_attn_wv, L0_attn_wr, L0_attn_wo, L0_attn_time_decay,
           L0_attn_time_first, L0_attn_mix_k, L0_attn_mix_v, L0_attn_mix_r, L0_xattn_Wq, L0_xattn_Wk,
           L0_xattn_Wv, L0_xattn_Wo, L0_ffn_Wr, L0_ffn_br, L0_ffn_W1, L0_ffn_b1, L0_ffn_W2, L0_ffn_b2):
    import numpy as np
    import concourse.bacc as bacc
    from concourse.bass_utils import run_bass_kernel_spmd

    f32 = np.float32
    ident = np.eye(P, dtype=f32)
    c, h = np.arange(P)[:, None], np.arange(QH)[None, :]
    qmask = ((c // HD) % QH == h).astype(f32) * f32(HD ** -0.5)
    r = np.arange(KT * P).reshape(KT, P).T[:, :, None]
    vmask = (r // M == np.arange(H)[None, None, :] % QH).astype(f32).reshape(P, KT * H)
    cols = np.stack([np.asarray(a).reshape(C) for a in
                     (L0_attn_time_decay, L0_attn_time_first, L0_attn_mix_k, L0_attn_mix_v, L0_attn_mix_r)], 1)
    b1 = np.asarray(L0_ffn_b1).reshape(NS, P).T
    pack = np.concatenate([ident, qmask, vmask, cols, np.asarray(L0_attn_wk).T, np.asarray(L0_attn_wv).T,
                           np.asarray(L0_attn_wr).T, np.asarray(L0_attn_wo).T, np.asarray(L0_xattn_Wq),
                           np.asarray(L0_xattn_Wo), np.asarray(L0_ffn_Wr), b1, np.asarray(L0_ffn_b2).T], 1)
    arrays = {
        "x": np.asarray(x).transpose(1, 0, 2),
        "ctxT": np.asarray(ctx_768).transpose(2, 0, 1),
        "mask": np.asarray(mask_BxS2_bf1).reshape(1, B * M).view(np.uint8),
        "pack": pack,
        "wkv96": np.concatenate([np.asarray(L0_xattn_Wk), np.asarray(L0_xattn_Wv)], 1),
        "br": np.asarray(L0_ffn_br).reshape(1, E),
        "w1": np.asarray(L0_ffn_W1).transpose(1, 0, 2).reshape(P, E * F),
        "w2": np.asarray(L0_ffn_W2).reshape(NS, P, C).transpose(1, 0, 2).reshape(P, NS * C),
    }
    arrays = {n: np.ascontiguousarray(a) for n, a in arrays.items()}
    nc = bacc.Bacc("TRN2", target_bir_lowering=False, num_devices=1)
    args = [nc.dram_tensor(n, a.shape, mybir.dt.from_np(a.dtype), kind="ExternalInput").ap()
            for n, a in arrays.items()]
    args.append(nc.dram_tensor("out", (T, B, C), F32, kind="ExternalOutput").ap())
    build(nc, *args)
    got = run_bass_kernel_spmd(nc, [arrays], core_ids=[0]).results[0]["out"]
    return np.ascontiguousarray(got.transpose(1, 0, 2))
```

```python
from contextlib import ExitStack

import concourse.bass as bass
from concourse import mybir

F32 = mybir.dt.float32
F32R = mybir.dt.float32r
U8 = mybir.dt.uint8
ALU = mybir.AluOpType
ACT = mybir.ActivationFunctionType
AX_X = mybir.AxisListType.X

P = 128
B, T, C = 16, 128, 128
SIZES = (4, 4, 4, 4)
G = len(SIZES)
START = [sum(SIZES[:g]) for g in range(G)]
CHUNKS = (2, 2, 4, 4, 4)
CSTART = [sum(CHUNKS[:c]) for c in range(len(CHUNKS))]
GB = max(SIZES + CHUNKS)
MIX_TICKS = (
    (0, 2, 3, 4, 5, 7, 7, 8, 9, 10, 11, 11, 14, 16, 17, 18, 19, 20, 20, 22, 24, 25, 27, 28, 29, 29),
    (0, 2, 3, 4, 5, 6, 7, 8, 9, 10, 11, 12, 14, 16, 17, 18, 19, 19, 20, 21, 23, 24, 26, 27, 28, 30),
)
FIRST_LAID = (15, 21)
ATTEND_TICKS = (-4, 1, 3, 5, 10, 12, 14, 15, 17, 18)
MIX_AT = (0, 16, 32, 62, 95)
ATTEND_AT = (32, 36, 48, 52, 67, 71, 75, 79, 99, 103, 107, 111, 131, 135, 139, 143)
EXPERTS_AT = (71, 103, 135, 167)
N = GB * T
TP = T + 1
NPAD = GB * TP
M, CTX = 77, 96
H, HD = 16, 8
QH = 4
NQ = H // QH
SQ = QH * M
KT = -(-SQ // P)
SP = KT * P
E, F = 8, 512
FT = F // P
NS = E * FT
NEWTON = 6
RAW = 2
HS = 2
HIDS = 4
CTX_RING = 3
PROBS = 3
HC = QH * HD
KS = 3 * HC + 1
KEYS_IN, QUERIES_IN = 16 * (3 + 1), 16 * 3
EPS = 1e-5
THRESH = 1e-9
NEG = -1e38
MASKED = 3.3895313892515355e38

PACK = {}
_at = 0
for _name, _n in (("ident", P), ("qmask", QH), ("vmask", KT * H), ("cols", 5), ("wkT", C), ("wvT", C),
                  ("wrT", C), ("woT", C), ("Wq", C), ("Wo", C), ("Wr", E), ("b1", NS), ("b2", E)):
    PACK[_name] = (_at, _at + _n)
    _at += _n
PACKED = _at


def mixing_steps(g, t):
    n = CHUNKS[g]
    half = min(n, 2)
    norm = [[("norm", k, g, b) for b in range(n)] for k in range(2)]
    stages = (
        [("stats", 0, g, None)], norm[0][0:half], norm[0][half:n], [("turn", 0, g, None)], [("key", g)],
        [("value", g), ("maximum", g)], [("receptance", g), ("exponent", g, 0), ("exponent", g, 1)],
        [("exponent", g, 2), ("exp", g, 0)], [("exponent", g, 3), ("exp", g, 1)], [("weighted", g), ("exp", g, 2)],
        [("scan_den", g), ("exp", g, 3)], [("scan_num", g), ("denominator", g)], [("numerator", g, 0)],
        [("numerator", g, 1)], [("receive", g)], [("inverse", g, 0)], [("inverse", g, 1)], [("inverse", g, 2)],
        [("inverse", g, 3)], [("rwkv", g)], [("mixed", g)], [("stats", 1, g, None)], norm[1][0:half],
        norm[1][half:n], [("turn", 1, g, None)], [("query", g)])
    return [st for at, sts in zip(MIX_TICKS[g > 1], stages) if at == t for st in sts]


def attention_steps(g, b, t):
    out = []
    turns = range(NQ)
    laid, scored, turned, weighed, heads, summed, normed, last, routed, found = ATTEND_TICKS
    if t - weighed in turns:
        out.append(("probs_v", g, NQ * b + turns.index(t - weighed)))
    i = START[g] + b
    if i < len(FIRST_LAID):
        laid = FIRST_LAID[i] - ATTEND_AT[i]
    elif i >= 3:
        laid = max(laid, ATTEND_AT[i - 3] - ATTEND_AT[i] + weighed + turns[-1])
    if t == laid:
        out.append(("context", g, b))
        out.append(("keys", g, b))
    if t - scored in turns:
        out.append(("scores", g, NQ * b + turns.index(t - scored)))
    if t - turned in turns:
        out.append(("turn_probs", g, NQ * b + turns.index(t - turned)))
    for tick, steps in ((heads, [("turn_heads", g, b)]), (summed, [("attended", g, b), ("stats", 2, g, b)]),
                        (normed, [("norm", 2, g, b)]), (last, [("turn", 2, g, b)])):
        if t == tick:
            out += steps
    if b == SIZES[g] - 1:
        if t == routed:
            out.append(("router", g))
        if 0 <= t - found <= NEWTON:
            out.append(("threshold", g, t - found))
    return out


DOWN_LAG = 3
GATE_LAG = 9
EXPERT_TICKS = NS + GATE_LAG - FT + 1


def expert_steps(g, t):
    out = []
    if 0 <= t - DOWN_LAG < NS:
        out.append(("down", g, t - DOWN_LAG))
    if 0 <= t < NS:
        out.append(("hidden", g, t))
    e, rest = divmod(t - GATE_LAG, FT)
    if rest == 0 and 0 <= e < E:
        out.append(("gated", g, e))
    return out


SPLIT_AT = (9, 13, 15, 17, 18, 23, 34, 36, 37, 40, 42, 44, 52, 54, 56, 58)
ORDER = {k: i for i, k in enumerate(("down", "probs_v", "context", "scores", "turn_probs", "hidden", "others",
                                     "gated"))}


def order(st):
    return ORDER.get(st[0], ORDER["others"])


LAGS = {("scalar", "scores"): 0.5, ("scalar", "turn_heads"): 0.7, ("vector", "exponent"): 0.5,
        ("vector", "attended"): -0.2, ("vector", "inverse"): -0.1, ("vector", "probs_v"): -0.3,
        ("vector", "context"): -0.1, ("gpsimd", "denominator"): 0.1, ("tensor", "turn_heads"): 0.2,
        ("tensor", "scores"): -0.1, ("gpsimd", "split"): -0.3, ("gpsimd", "exponent"): -0.3,
        ("vector", "norm"): -0.1}


def plan():
    steps, at = [], {}
    for t in range(EXPERTS_AT[-1] + EXPERT_TICKS):
        tick = [("split", j) for j in range(2 * E) if t == SPLIT_AT[j]]
        for g in range(G):
            tick += expert_steps(g, t - EXPERTS_AT[g])
            for b in range(SIZES[g]):
                tick += attention_steps(g, b, t - ATTEND_AT[START[g] + b])
        for c in range(len(CHUNKS)):
            tick += mixing_steps(c, t - MIX_AT[c])
        steps += sorted(tick, key=order)
        at.update({st: t + order(st) / 10 for st in tick})
    return steps, at


def build(nc, x, ctxT, mask, pack, wkv96, br, w1, w2, out):
    steps, at = plan()

    def program(engine):
        return sorted(steps, key=lambda st: at[st] + LAGS.get((engine, st[0]), 0))

    nth = {}
    seen = {}
    for st in steps:
        seen[st[0]] = seen.get(st[0], 0) + 1
        nth[st] = seen[st[0]]
    last_turn, last = {}, None
    for st in steps:
        if st[0] in ("norm", "turn") and st[1] < 2:
            last_turn[st] = last
            if st[0] == "turn":
                last = st
    SHARED = ("turn", "key", "value", "receptance", "mixed", "query", "context", "probs_v",
              "turn_heads", "attended", "router", "gated")
    shared = {st: i for i, st in enumerate(s for s in steps if s[0] in SHARED)}

    with ExitStack() as ctx:
        def sb(name, shape, dt=F32):
            return ctx.enter_context(nc.sbuf_tensor(name, shape, dt))

        def ps(name):
            return ctx.enter_context(nc.psum_tensor(name, [P, 512], F32))

        def sem(name):
            return ctx.enter_context(nc.semaphore(name))

        resid = sb("resid", [P, B, C])
        pk = sb("pk", [P, PACKED])
        w96 = sb("w96", [CTX, 2 * C])
        ctx_sb = sb("ctx_sb", [CTX, B, M])
        br_sb = sb("br_sb", [1, E])
        w_raw = sb("w_raw", [P, RAW, F])
        w1_hi = sb("w1_hi", [P, E * F], F32R)
        w1_lo = sb("w1_lo", [P, E * F], F32R)
        w2_hi = sb("w2_hi", [P, NS * C], F32R)
        w2_lo = sb("w2_lo", [P, NS * C], F32R)
        mask_u8 = sb("mask_u8", [P, B * M], U8)
        mask_row = sb("mask_row", [P, 2, M], F32R)
        ones_f = sb("ones_f", [1, P])
        half_neg = sb("half_neg", [P, GB])
        mix_c = sb("mix_c", [P, 3])
        w_now = sb("w_now", [P, 3, C])
        w_before = sb("w_before", [P, 3, C])
        decay_w = sb("decay_w", [P, 1])
        decay_row = sb("decay_row", [P, NPAD])
        bn = sb("bn", [P, B, 6])
        mv = sb("mv", [P, 3, B, 2])
        var_e = sb("var_e", [P, 3, B])
        rstd = sb("rstd", [P, 3, B])
        xn_mix = sb("xn_mix", [P, max(CHUNKS), C])
        xn_attend = sb("xn_attend", [P, 2, C])
        xT1 = sb("xT1", [P, NPAD])
        xT2 = sb("xT2", [P, N])
        xT3 = sb("xT3", [P, N])
        x_hi = sb("x_hi", [P, 2, N], F32R)
        x_lo = sb("x_lo", [P, 2, N], F32R)
        k_sb = sb("k_sb", [P, NPAD])
        v_sb = sb("v_sb", [P, NPAD])
        er = sb("er", [P, N])
        mx = sb("mx", [P, NPAD])
        ex = sb("ex", [P, 4, NPAD])
        den = ex[:, 1, :]
        ev = sb("ev", [P, NPAD])
        ta = sb("ta", [P, N])
        tb = sb("tb", [P, N])
        tc = sb("tc", [P, N])
        q_parts = sb("q_parts", [P, 2, N], F32R)
        q_hi, q_lo = q_parts[:, 0, :], q_parts[:, 1, :]
        q_stack = sb("q_stack", [KS, NQ, N], F32R)
        k_stack = sb("k_stack", [KS, 2, NQ, SQ], F32R)
        ctx4 = sb("ctx4", [CTX, CTX_RING, SP])
        kbd = sb("kbd", [P, SQ])
        k_parts = sb("k_parts", [P, 2, SQ], F32R)
        k_hi, k_lo = k_parts[:, 0, :], k_parts[:, 1, :]
        vbd = sb("vbd", [P, 3, KT * H * (HD + 1)])
        smax = sb("smax", [P, 2, QH])
        prob = sb("prob", [P, PROBS, SP])
        probT = sb("probT", [P, 3, SP])
        rsum = sb("rsum", [P, 2, QH])
        heads = sb("heads", [P, 2, C])
        headsT = sb("headsT", [P, 2, C])
        xs = sb("xs", [P, GB, E])
        diff = sb("diff", [P, GB, E])
        above = sb("above", [P, GB, 2, E])
        top = sb("top", [P, GB])
        tau = sb("tau", [P, GB])
        sums = sb("sums", [P, GB, 2])
        inv = sb("inv", [P, GB])
        gates = sb("gates", [P, 2, GB, E])
        hid = sb("hid", [P, HS, N])
        hid_hi = sb("hid_hi", [P, HIDS, N], F32R)
        hid_lo = sb("hid_lo", [P, HIDS, N], F32R)
        yT = sb("yT", [P, 2, N])

        bank_z = [ps("bank_z0"), ps("bank_z1")]
        bank_y = ps("bank_y")
        bank_s = [ps("bank_s0"), ps("bank_s1")]
        bank_p = ps("bank_p")
        bank_m = [ps("bank_m0"), ps("bank_m1")]

        x_in = [sem(f"x_in{c}") for c in range(len(CHUNKS))]
        pack_in, ctx_in, small_in = sem("pack_in"), sem("ctx_in"), sem("small_in")
        w_in = [sem(f"w_in{j}") for j in range(2 * E)]
        w_hi_ready, w_split = sem("w_hi_ready"), sem("w_split")
        pool_step = sem("pool_step")
        pool_const, dve_const, act_const = sem("pool_const"), sem("dve_const"), sem("act_const")
        ones_ready = sem("ones_ready")
        dve_step = sem("dve_step")
        stats_ready, rstd_ready, normed = sem("stats_ready"), sem("rstd_ready"), sem("normed")
        full = [sem("full0"), sem("full1")]
        freed = [sem("freed0"), sem("freed1")]
        er_ready = sem("er_ready")
        exponents_ready, exps_ready, rwkv_ready = sem("exponents_ready"), sem("exps_ready"), sem("rwkv_ready")
        maximum_ready, exponent1_ready = sem("maximum_ready"), sem("exponent1_ready")
        den_ready, denominator_ready = sem("den_ready"), sem("denominator_ready")
        inverted = sem("inverted")
        mixing_read = sem("mixing_read")
        ctx4_ready, kbd_ready = sem("ctx4_ready"), sem("kbd_ready")
        k_hi_ready, k_lo_ready, k_in = sem("k_hi_ready"), sem("k_lo_ready"), [sem("k_in0"), sem("k_in1")]
        q_hi_ready, q_in = sem("q_hi_ready"), sem("q_in")
        k_out, q_out = sem("k_out"), sem("q_out")
        scores_full, scores_read = sem("scores_full"), sem("scores_read")
        exp_ready, probs_turned, probT_ready = sem("exp_ready"), sem("probs_turned"), sem("probT_ready")
        heads_ready = sem("heads_ready")
        gates_ready = sem("gates_ready")
        hi_ready, lo_ready = sem("hi_ready"), sem("lo_ready")
        z_full, hid_ready, hid_split, hid_used = sem("z_full"), sem("hid_ready"), sem("hid_split"), sem("hid_used")
        y_full, y_ready = sem("y_full"), sem("y_ready")
        stored = sem("stored")

        def part(name):
            return pk[:, PACK[name][0]:PACK[name][1]]

        ident = part("ident")
        cols = part("cols")
        first = cols[:, 1:2]

        def now(t):
            return t.rearrange("p (b t) -> p b t", t=TP)[:, :, 1:TP]

        def before(t):
            return t.rearrange("p (b t) -> p b t", t=TP)[:, :, 0:T]

        def pads(t):
            return t.rearrange("p (b t) -> p b t", t=TP)[:, :, 0:1]

        def by_batch(t):
            return t.rearrange("p (b t) -> p b t", t=T)

        def tok(g):
            return SIZES[g] * T

        def ctok(c):
            return CHUNKS[c] * T

        def npad(c):
            return CHUNKS[c] * TP

        def shared_bank(st):
            return bank_m[shared[st] % 2]

        def wait_full(eng, st):
            eng.wait_ge(full[shared[st] % 2], shared[st] // 2 + 1)

        def wait_moved(eng, st):
            eng.wait_ge(freed[shared[st] % 2], shared[st] // 2 + 1)

        def wait_bank(eng, st):
            if shared[st] >= 2:
                eng.wait_ge(freed[shared[st] % 2], shared[st] // 2)

        def fill_done(ins, st):
            ins.then_inc(full[shared[st] % 2], 1)

        def moved(ins, st):
            ins.then_inc(freed[shared[st] % 2], 1)

        def wait_down(eng, i):
            if i % FT == FT - 1:
                eng.wait_ge(y_full, i // FT + 1)
            else:
                eng.wait_ge(hid_used, i // FT * (FT - 1) + i % FT + 1)

        def wait_stacked(eng, i):
            eng.wait_ge(k_in[i % 2], KEYS_IN * (i // 2 + 1))

        def batches(k, g, b):
            start, size = (START[g], SIZES[g]) if k == 2 else (CSTART[g], CHUNKS[g])
            return range(start, start + size) if b is None else range(start + b, start + b + 1)

        def group_of(i):
            g = max(g for g in range(G) if START[g] <= i)
            return g, i - START[g]

        def chunk_of(i):
            c = max(c for c in range(len(CHUNKS)) if CSTART[c] <= i)
            return c, i - CSTART[c]

        def unit(n):
            g, b = group_of(n // NQ)
            return g, NQ * b + n % NQ

        k_spill = nc.dram_tensor("k_spill", (B, 2, P, SQ), F32, kind="Internal").ap()
        q_spill = nc.dram_tensor("q_spill", (len(CHUNKS), 2, P, N), F32, kind="Internal").ap()

        block = ctx.enter_context(nc.Block())

        @block.sync
        def _(sp):
            sp.dma_start(resid[:, 0:CHUNKS[0], :], x[:, 0:CHUNKS[0], :]).then_inc(x_in[0], 16)
            sp.dma_start(pk[:, :], pack).then_inc(pack_in, 16)
            sp.dma_start(w96[:, :], wkv96).then_inc(ctx_in, 16)
            sp.dma_start(ctx_sb[:, :, :], ctxT).then_inc(ctx_in, 16)
            sp.dma_start(br_sb[:, :], br).then_inc(small_in, 16)
            sp.dma_start(mask_u8[:, :], mask.broadcast_to([P, B * M])).then_inc(small_in, 16)
            for c in range(1, len(CHUNKS)):
                at = slice(CSTART[c], CSTART[c] + CHUNKS[c])
                sp.dma_start(resid[:, at, :], x[:, at, :]).then_inc(x_in[c], 16)

            def load(j):
                e, second = divmod(j, 2)
                if j >= RAW:
                    sp.wait_ge(w_split, j - RAW + 1)
                sp.dma_start(w_raw[:, j % RAW, :], (w1, w2)[second][:, e * F:(e + 1) * F]).then_inc(w_in[j], 16)

            for j in range(RAW):
                load(j)
            for st in program("sync"):
                if st[0] == "split" and st[1] + RAW < 2 * E:
                    load(st[1] + RAW)
                if st[0] == "keys":
                    i = nth[st] - 1
                    dst = k_stack[:, i % 2, :, :].bitcast(F32)
                    if i >= 2:
                        sp.wait_ge(scores_full, NQ * (i - 1))
                    sp.wait_ge(k_lo_ready, i + 1)
                    sp.dma_start(k_spill[i].rearrange("h c n -> c h n"), k_parts[:, :, :].bitcast(F32))\
                        .then_inc(k_out, 16)
                    sp.wait_ge(k_out, 16 * (i + 1))
                    for n, h in enumerate((0, 1, 0)):
                        sp.dma_start(dst[n * HC:(n + 1) * HC, :, :],
                                     k_spill[i, h].rearrange("(q p) n -> p q n", p=HC)).then_inc(k_in[i % 2], 16)
                    wait_moved(sp, ("context", st[1], st[2]))
                    sp.dma_start(dst[3 * HC:KS, :, :].rearrange("p q (h m) -> p (q h) m", m=M),
                                 mask_row[3 * HC:KS, i % 2:i % 2 + 1, :].bitcast(F32)
                                 .broadcast_to([1, NQ * QH, M])).then_inc(k_in[i % 2], 16)
                if st[0] == "query":
                    c, n = st[1], ctok(st[1])
                    if c >= 1:
                        sp.wait_ge(scores_full, NQ * CSTART[c])
                    wait_moved(sp, st)
                    sp.dma_start(q_spill[c, :, :, 0:n].rearrange("h c n -> c h n"), q_parts[:, :, 0:n].bitcast(F32))\
                        .then_inc(q_out, 16)
                    sp.wait_ge(q_out, 16 * (c + 1))
                    for k, h in enumerate((0, 0, 1)):
                        sp.dma_start(q_stack[k * HC:(k + 1) * HC, :, 0:n].bitcast(F32),
                                     q_spill[c, h, :, 0:n].rearrange("(q p) n -> p q n", p=HC)).then_inc(q_in, 16)
                if st[0] == "gated" and st[2] == E - 1:
                    wait_moved(sp, st)
                    at = slice(START[st[1]], START[st[1]] + SIZES[st[1]])
                    sp.dma_start(out[:, at, :], resid[:, at, :]).then_inc(stored, 16)
            sp.wait_ge(stored, 16 * G)

        @block.gpsimd
        def _(pool):
            chain = [0]

            def link(ins):
                chain[0] += 1
                ins.then_inc(pool_step, 1)
                pool.wait_ge(pool_step, chain[0])

            nc.gpsimd.memset(half_neg[:, :], -0.5)
            nc.gpsimd.memset(ctx4[:, :, SQ:SP], 0.0)
            nc.gpsimd.memset(ones_f[:, :], 1.0)
            nc.gpsimd.memset(prob[:, :, SQ:SP], 0.0)
            for t, value in ((xT1[:, :], 0.0), (ex[:, 0, :], 0.0), (ex[:, 1, :], 0.0),
                             (ev[:, :], 0.0), (k_sb[:, :], NEG)):
                ins = nc.gpsimd.memset(pads(t), value)
            ins.then_inc(pool_const, 1)
            pool.wait_ge(pool_const, 1)

            def split(j):
                e, second = divmod(j, 2)
                at = slice(e * F, (e + 1) * F)
                pool.wait_ge(w_hi_ready, j + 1)
                nc.gpsimd.tensor_tensor((w1_lo, w2_lo)[second][:, at], w_raw[:, j % RAW, :],
                                        (w1_hi, w2_hi)[second][:, at].bitcast(F32), ALU.subtract)\
                    .then_inc(w_split, 1)

            def hidden(st):
                i, n = nth[st] - 1, tok(st[1])
                pool.wait_ge(hid_ready, i + 1)
                if i >= HIDS:
                    wait_down(pool, i - HIDS)
                nc.gpsimd.tensor_tensor(hid_lo[:, i % HIDS, 0:n], hid[:, i % HS, 0:n],
                                        hid_hi[:, i % HIDS, 0:n].bitcast(F32), ALU.subtract).then_inc(hid_split, 1)

            def stats(st):
                _, k, g, b = st
                pool.wait_ge(stats_ready, nth[st])
                at = batches(k, g, b)
                lo, hi = at[0], at[-1] + 1
                v = var_e[:, k, lo:hi]
                link(nc.gpsimd.tensor_scalar(v, mv[:, k, lo:hi, 1], EPS, 1.0, ALU.add, ALU.mult))
                nc.gpsimd.tensor_tensor(rstd[:, k, lo:hi], v, half_neg[:, 0:hi - lo], ALU.pow)\
                    .then_inc(rstd_ready, 1)

            def replicate(i):
                if i == 0:
                    pool.wait_ge(ctx_in, 32)
                if i >= CTX_RING:
                    wait_full(pool, ("context", *group_of(i - CTX_RING)))
                nc.gpsimd.tensor_copy(ctx4[:, i % CTX_RING, 0:SQ].rearrange("p (h m) -> p h m", m=M),
                                      ctx_sb[:, i:i + 1, :].broadcast_to([CTX, QH, M]))\
                    .then_inc(ctx4_ready, 1)

            def keys(st):
                i = nth[st] - 1
                pool.wait_ge(k_hi_ready, i + 1)
                if i >= 1:
                    pool.wait_ge(k_out, 16 * i)
                nc.gpsimd.tensor_tensor(k_lo[:, :], kbd[:, :], k_hi[:, :].bitcast(F32), ALU.subtract)\
                    .then_inc(k_lo_ready, 1)

            def exponent1(g):
                n = npad(g)
                pool.wait_ge(maximum_ready, g + 1)
                nc.gpsimd.tensor_tensor(now(ex[:, 1, 0:n]), now(k_sb[:, 0:n]), now(mx[:, 0:n]), ALU.subtract)\
                    .then_inc(exponent1_ready, 1)

            def denominator(g):
                n, m = npad(g), ctok(g)
                b, c = by_batch(tb[:, 0:m]), by_batch(tc[:, 0:m])
                e1, e2 = now(ex[:, 2, 0:n]), now(ex[:, 3, 0:n])
                if g >= 1:
                    pool.wait_ge(rwkv_ready, g)
                wait_moved(pool, ("value", g))
                pool.wait_ge(exps_ready, 4 * g + 4)
                nc.gpsimd.tensor_tensor(b, e2, now(v_sb[:, 0:n]), ALU.mult)
                pool.wait_ge(den_ready, g + 1)
                link(nc.gpsimd.tensor_tensor(c, e1, before(den[:, 0:n]), ALU.mult))
                nc.gpsimd.tensor_tensor(c, c, e2, ALU.add).then_inc(denominator_ready, 1)

            for st in program("gpsimd"):
                if st[0] == "exponent" and st[2] == 1:
                    exponent1(st[1])
                if st[0] == "denominator":
                    denominator(st[1])
                if st[0] == "stats":
                    stats(st)
                if st[0] == "stats" and st[1] == 0 and st[2] == 0:
                    for i in range(CTX_RING):
                        replicate(i)
                if st[0] == "context" and START[st[1]] + st[2] + CTX_RING < B:
                    replicate(START[st[1]] + st[2] + CTX_RING)
                if st[0] == "split":
                    split(st[1])
                if st[0] == "hidden":
                    hidden(st)
                if st[0] == "keys":
                    keys(st)

        @block.scalar
        def _(act):
            act.wait_ge(pack_in, 16)
            nc.scalar.activation(decay_w[:, :], cols[:, 0:1], ACT.Exp).then_inc(act_const, 1)
            act.wait_ge(pool_const, 1)

            def split(st):
                j = st[1]
                e, second = divmod(j, 2)
                act.wait_ge(w_in[j], 16)
                nc.scalar.activation((w1_hi, w2_hi)[second][:, e * F:(e + 1) * F], w_raw[:, j % RAW, :], ACT.Copy)\
                    .then_inc(w_hi_ready, 1)

            def turn(st):
                _, k, g, b = st
                wait_full(act, st)
                src = shared_bank(st)
                if k == 0:
                    if g >= 1:
                        wait_full(act, ("receptance", g - 1))
                    moved(nc.scalar.activation(now(xT1[:, 0:npad(g)]), by_batch(src[:, 0:ctok(g)]), ACT.Copy),
                          st)
                elif k == 1:
                    if g >= 1:
                        wait_full(act, ("query", g - 1))
                    moved(nc.scalar.activation(xT2[:, 0:ctok(g)], src[:, 0:ctok(g)], ACT.Copy), st)
                else:
                    at = slice(b * T, b * T + T)
                    if g >= 1:
                        wait_full(act, ("router", g - 1))
                    if g >= 2:
                        act.wait_ge(z_full, NS * (g - 1))
                    nc.scalar.activation(x_hi[:, g % 2, at], src[:, 0:T], ACT.Copy).then_inc(hi_ready, 1)
                    moved(nc.scalar.activation(xT3[:, at], src[:, 0:T], ACT.Copy), st)

            def key(st):
                g = st[1]
                wait_full(act, st)
                if g >= 1:
                    act.wait_ge(mixing_read, g)
                moved(nc.scalar.activation(now(k_sb[:, 0:npad(g)]), by_batch(shared_bank(st)[:, 0:ctok(g)]),
                                           ACT.Copy), st)

            def value(st):
                g = st[1]
                wait_full(act, st)
                moved(nc.scalar.activation(now(v_sb[:, 0:npad(g)]), by_batch(shared_bank(st)[:, 0:ctok(g)]),
                                           ACT.Copy), st)

            def receptance(st):
                wait_full(act, st)
                n = ctok(st[1])
                moved(nc.scalar.activation(er[:, 0:n], shared_bank(st)[:, 0:n], ACT.Exp, scale=-1.0), st)

            def exp(st):
                _, g, i = st
                if i == 1:
                    act.wait_ge(exponent1_ready, g + 1)
                else:
                    act.wait_ge(exponents_ready, 2 * g + min(i, 2) // 2 + 1)
                e = now(ex[:, i, 0:npad(g)])
                nc.scalar.activation(e, e, ACT.Exp).then_inc(exps_ready, 1)

            def query(st):
                g = st[1]
                wait_full(act, st)
                if g >= 1:
                    act.wait_ge(q_out, 16 * g)
                n = ctok(g)
                nc.scalar.activation(q_hi[:, 0:n], shared_bank(st)[:, 0:n], ACT.Copy).then_inc(q_hi_ready, 1)

            def keys(st):
                i = nth[st] - 1
                act.wait_ge(kbd_ready, i + 1)
                if i >= 1:
                    act.wait_ge(k_out, 16 * i)
                nc.scalar.activation(k_hi[:, :], kbd[:, :], ACT.Copy).then_inc(k_hi_ready, 1)

            def scores(st):
                u = nth[st] - 1
                act.wait_ge(scores_read, u + 1)
                pr = prob[:, u % PROBS, 0:SQ]
                nc.scalar.activation(pr, pr, ACT.Exp).then_inc(exp_ready, 1)

            def turn_probs(st):
                u = nth[st] - 1
                act.wait_ge(probs_turned, u + 1)
                if u >= 3:
                    wait_full(act, ("probs_v", *unit(u - 3)))
                nc.scalar.activation(probT[:, u % 3, :], bank_p[:, 0:SP], ACT.Copy).then_inc(probT_ready, 1)

            def turn_heads(st):
                i = nth[st] - 1
                wait_full(act, st)
                if i >= 2:
                    wait_full(act, ("attended", *group_of(i - 2)))
                moved(nc.scalar.activation(headsT[:, i % 2, :], shared_bank(st)[:, 0:C], ACT.Copy), st)

            def router(st):
                g = st[1]
                wait_full(act, st)
                if g >= 1:
                    act.wait_ge(gates_ready, g)
                n = SIZES[g]
                moved(nc.scalar.activation(xs[:, 0:n, :], shared_bank(st)[:, 0:n * E]
                                           .rearrange("p (b e) -> p b e", e=E), ACT.Copy, scale=0.5), st)

            def hidden(st):
                i, s, n = nth[st] - 1, st[2], tok(st[1])
                act.wait_ge(z_full, i + 1)
                if i >= HIDS:
                    wait_down(act, i - HIDS)
                z, bias = bank_z[i % 2][:, 0:n], part("b1")[:, s:s + 1]
                nc.scalar.activation(hid_hi[:, i % HIDS, 0:n], z, ACT.Relu, bias=bias)
                if i >= HS:
                    act.wait_ge(hid_split, i - HS + 1)
                nc.scalar.activation(hid[:, i % HS, 0:n], z, ACT.Relu, bias=bias).then_inc(hid_ready, 1)

            def down(st):
                _, g, s = st
                if s % FT < FT - 1:
                    return
                e = s // FT
                i = E * g + e
                act.wait_ge(y_full, i + 1)
                if i >= 2:
                    wait_full(act, ("gated", (i - 2) // E, (i - 2) % E))
                n = tok(g)
                nc.scalar.activation(yT[:, i % 2, 0:n], bank_y[:, 0:n], ACT.Identity,
                                     bias=part("b2")[:, e:e + 1]).then_inc(y_ready, 1)

            run = {"split": split, "turn": turn, "key": key, "value": value, "receptance": receptance, "exp": exp,
                   "query": query, "keys": keys, "scores": scores, "turn_probs": turn_probs,
                   "turn_heads": turn_heads, "router": router, "hidden": hidden, "down": down}
            for st in program("scalar"):
                if st[0] in run:
                    run[st[0]](st)

        @block.vector
        def _(dve):
            chain = [0]

            def link(ins):
                chain[0] += 1
                ins.then_inc(dve_step, 1)
                dve.wait_ge(dve_step, chain[0])

            v = nc.vector
            v.memset(q_stack[3 * HC:KS, :, :].bitcast(F32), 1.0).then_inc(ones_ready, 1)

            def weights():
                v.memset(decay_row[:, :], 0.0).then_inc(dve_step, 1)
                chain[0] += 1
                dve.wait_ge(pack_in, 16)
                dve.wait_ge(pool_const, 1)
                link(v.tensor_scalar(mix_c[:, :], cols[:, 2:5], -1.0, 1.0, ALU.mult, ALU.add))
                for i, name in enumerate(("wkT", "wvT", "wrT")):
                    v.tensor_scalar(w_now[:, i, :], part(name), cols[:, 2 + i:3 + i], None, ALU.mult)
                    ins = v.tensor_scalar(w_before[:, i, :], part(name), mix_c[:, i:i + 1], None, ALU.mult)
                ins.then_inc(dve_const, 1)
                dve.wait_ge(act_const, 1)
                v.tensor_scalar(now(decay_row[:, :]), now(decay_row[:, :]), decay_w[:, 0:1], None, ALU.subtract)\
                    .then_inc(dve_step, 1)
                v.memset(pads(decay_row[:, :]), NEG).then_inc(dve_step, 1)
                chain[0] += 2

            def consts():
                dve.wait_ge(small_in, 32)
                for i in range(3):
                    v.tensor_copy(vbd[:, i, :].rearrange("p (k d) -> p k d", d=HD + 1)[:, :, HD], part("vmask"))

            def stats(st):
                _, k, g, b = st
                if k == 0:
                    dve.wait_ge(x_in[g], 16)
                for i in batches(k, g, b):
                    ins = v.bn_stats(bn[:, i, :], resid[:, i, :])
                link(ins)
                for i in batches(k, g, b):
                    ins = v.bn_aggr(mv[:, k, i, :], bn[:, i, :])
                ins.then_inc(stats_ready, 1)
                if (k, g) == (0, 0):
                    weights()

            def norm(st):
                _, k, g, b = st
                dve.wait_ge(rstd_ready, nth[("stats", k, g, b if k == 2 else None)])
                i = batches(k, g, b)[0]
                if k == 2:
                    if i >= 2:
                        g2, b2 = group_of(i - 2)
                        wait_full(dve, ("turn", 2, g2, b2))
                    dst = xn_attend[:, i % 2, :]
                else:
                    if b == 0 and last_turn[st] is not None:
                        wait_full(dve, last_turn[st])
                    dst = xn_mix[:, b, :]
                v.tensor_scalar(dst, resid[:, i, :], mv[:, k, i, 0:1], rstd[:, k, i:i + 1],
                                ALU.subtract, ALU.mult).then_inc(normed, 1)

            def turn(st):
                _, k, g, b = st
                if k == 2:
                    wait_moved(dve, st)
                    if g >= 2:
                        dve.wait_ge(z_full, NS * (g - 1))
                    at = slice(b * T, b * T + T)
                    v.tensor_tensor(x_lo[:, g % 2, at], xT3[:, at], x_hi[:, g % 2, at].bitcast(F32),
                                    ALU.subtract).then_inc(lo_ready, 1)

            def maximum(st):
                g = st[1]
                n = npad(g)
                wait_moved(dve, ("key", g))
                if g == 0:
                    dve.wait_ge(dve_step, chain[0])
                v.tensor_tensor_scan(mx[:, 0:n], decay_row[:, 0:n], k_sb[:, 0:n], NEG, ALU.add, ALU.max)\
                    .then_inc(maximum_ready, 1)
                dve.wait_ge(maximum_ready, g + 1)

            def exponent(st):
                _, g, i = st
                n = npad(g)
                old, new = before(mx[:, 0:n]), now(mx[:, 0:n])
                e, a = now(ex[:, i, 0:n]), by_batch(ta[:, 0:ctok(g)])
                if i == 0:
                    v.scalar_tensor_tensor(e, old, decay_w[:, 0:1], new, ALU.subtract, ALU.subtract)\
                        .then_inc(exponents_ready, 1)
                elif i == 2:
                    if g >= 1:
                        wait_full(dve, ("mixed", g - 1))
                    link(v.scalar_tensor_tensor(a, now(k_sb[:, 0:n]), first, old, ALU.add, ALU.subtract))
                elif i == 3:
                    v.tensor_scalar(now(ex[:, 2, 0:n]), a, -1.0, 0.0, ALU.mult, ALU.min)
                    v.tensor_scalar(e, a, 0.0, None, ALU.min).then_inc(exponents_ready, 1)

            def weighted(st):
                g = st[1]
                n = npad(g)
                dve.wait_ge(exps_ready, 4 * g + 2)
                wait_moved(dve, ("value", g))
                link(v.tensor_tensor(now(ev[:, 0:n]), now(ex[:, 1, 0:n]), now(v_sb[:, 0:n]), ALU.mult))

            def scan_den(st):
                n = npad(st[1])
                v.tensor_tensor_scan(den[:, 0:n], ex[:, 0, 0:n], ex[:, 1, 0:n], 0.0, ALU.mult, ALU.add)\
                    .then_inc(den_ready, 1)

            def scan_num(st):
                n = npad(st[1])
                link(v.tensor_tensor_scan(ev[:, 0:n], ex[:, 0, 0:n], ev[:, 0:n], 0.0, ALU.mult, ALU.add))

            def numerator(st):
                _, g, i = st
                n, m = npad(g), ctok(g)
                a = by_batch(ta[:, 0:m])
                if i == 0:
                    dve.wait_ge(exps_ready, 4 * g + 3)
                    link(v.tensor_tensor(a, now(ex[:, 2, 0:n]), before(ev[:, 0:n]), ALU.mult))
                else:
                    dve.wait_ge(denominator_ready, g + 1)
                    link(v.tensor_tensor(a, a, by_batch(tb[:, 0:m]), ALU.add))

            def receive(st):
                g = st[1]
                m = ctok(g)
                wait_moved(dve, ("receptance", g))
                v.scalar_tensor_tensor(tb[:, 0:m], er[:, 0:m], 1.0, tc[:, 0:m], ALU.add, ALU.mult)\
                    .then_inc(mixing_read, 1)

            def inverse(st):
                _, g, i = st
                m = ctok(g)
                dve.wait_ge(mixing_read, g + 1)
                at = slice(i * m // 4, (i + 1) * m // 4)
                v.reciprocal(tc[:, at], tb[:, at]).then_inc(inverted, 1)

            def rwkv_(st):
                g = st[1]
                m = ctok(g)
                dve.wait_ge(inverted, 4 * (g + 1))
                v.tensor_tensor(ta[:, 0:m], ta[:, 0:m], tc[:, 0:m], ALU.mult).then_inc(rwkv_ready, 1)

            def mixed(st):
                g = st[1]
                wait_full(dve, st)
                r = resid[:, CSTART[g]:CSTART[g] + CHUNKS[g], :]
                moved(v.tensor_tensor(r, r, by_batch(shared_bank(st)[:, 0:ctok(g)]), ALU.add), st)
                wait_moved(dve, st)

            def query(st):
                g, n = st[1], ctok(st[1])
                dve.wait_ge(q_hi_ready, g + 1)
                if g >= 1:
                    dve.wait_ge(q_out, 16 * g)
                moved(v.tensor_tensor(q_lo[:, 0:n], shared_bank(st)[:, 0:n], q_hi[:, 0:n].bitcast(F32),
                                      ALU.subtract), st)

            def context(st):
                i = nth[st] - 1
                if i == 0:
                    consts()
                if i >= 2:
                    wait_stacked(dve, i - 2)
                row = slice(3 * HC, KS)
                v.tensor_scalar(mask_row[row, i % 2, :], mask_u8[row, i * M:(i + 1) * M], -1.0, MASKED,
                                ALU.add, ALU.mult)
                wait_full(dve, st)
                if i >= 1:
                    dve.wait_ge(k_lo_ready, i)
                src = shared_bank(st)
                v.tensor_tensor(kbd[:, :].rearrange("p (h m) -> p h m", m=M),
                                src[:, 0:M].rearrange("p (o m) -> p o m", o=1).broadcast_to([P, QH, M]),
                                part("qmask").rearrange("p (h o) -> p h o", o=1).broadcast_to([P, QH, M]),
                                ALU.mult).then_inc(kbd_ready, 1)
                if i >= 3:
                    wait_full(dve, ("probs_v", *unit(NQ * (i - 3) + NQ - 1)))
                moved(v.tensor_tensor(
                    vbd[:, i % 3, :].rearrange("p (k d) -> p k d", d=HD + 1)[:, :, 0:HD],
                    src[:, P:P + KT * C].rearrange("p (k d) -> p k d", d=HD),
                    part("vmask").rearrange("p (k o) -> p k o", o=1).broadcast_to([P, KT * H, HD]),
                    ALU.mult), st)

            def scores(st):
                u = nth[st] - 1
                dve.wait_ge(scores_full, u + 1)
                s = bank_s[u % 2][:, 0:SQ].rearrange("p (h m) -> p h m", m=M)
                link(v.tensor_reduce(smax[:, u % 2, :], s, AX_X, ALU.max))
                if u >= PROBS:
                    dve.wait_ge(probs_turned, u - PROBS + 1)
                v.tensor_tensor(prob[:, u % PROBS, 0:SQ].rearrange("p (h m) -> p h m", m=M), s,
                                smax[:, u % 2, :].rearrange("p (h o) -> p h o", o=1).broadcast_to([P, QH, M]),
                                ALU.subtract).then_inc(scores_read, 1)

            def probs_v(st):
                _, g, u = st
                wait_full(dve, st)
                o = shared_bank(st)[:, 0:QH * (HD + 1)].rearrange("p (h d) -> p h d", d=HD + 1)
                i = START[g] + u // NQ
                rs = rsum[:, u % 2, :].rearrange("p (h o) -> p h o", o=1)
                link(v.reciprocal(rs, o[:, :, HD:HD + 1]))
                if u % NQ == 0 and i >= 2:
                    wait_full(dve, ("turn_heads", *group_of(i - 2)))
                q = u % NQ
                moved(v.tensor_tensor(heads[:, i % 2, q * QH * HD:(q + 1) * QH * HD]
                                      .rearrange("p (h d) -> p h d", d=HD),
                                      o[:, :, 0:HD], rs.broadcast_to([P, QH, HD]), ALU.mult), st)

            def attended(st):
                _, g, b = st
                wait_full(dve, st)
                r = resid[:, START[g] + b, :]
                moved(v.tensor_tensor(r, r, shared_bank(st)[:, 0:C], ALU.add), st)
                wait_moved(dve, st)

            def wide(t, n):
                return t.rearrange("p (b o) -> p b o", o=1).broadcast_to([P, n, E])

            def router(st):
                g = st[1]
                n = SIZES[g]
                wait_moved(dve, st)
                link(v.tensor_reduce(top[:, 0:n], xs[:, 0:n, :], AX_X, ALU.max))
                v.tensor_tensor(xs[:, 0:n, :], xs[:, 0:n, :], wide(top[:, 0:n], n), ALU.subtract)
                link(v.memset(tau[:, 0:n], -1.0))

            def threshold(st):
                _, g, i = st
                n = SIZES[g]
                d, a, a2 = diff[:, 0:n, :], above[:, 0:n, 0, :], above[:, 0:n, 1, :]
                t, s1, s2, iv = tau[:, 0:n], sums[:, 0:n, 0], sums[:, 0:n, 1], inv[:, 0:n]
                link(v.tensor_tensor(d, xs[:, 0:n, :], wide(t, n), ALU.subtract))
                v.tensor_scalar(a, d, 0.0, None, ALU.max)
                link(v.scalar_tensor_tensor(a2, d, 0.0, d, ALU.max, ALU.mult))
                link(v.tensor_reduce(sums[:, 0:n, :], above[:, 0:n, :, :], AX_X, ALU.add))
                if i < NEWTON:
                    link(v.reciprocal(iv, s1))
                    link(v.scalar_tensor_tensor(iv, s2, -1.0, iv, ALU.add, ALU.mult))
                    link(v.scalar_tensor_tensor(t, iv, 0.5, t, ALU.mult, ALU.add))
                else:
                    link(v.reciprocal(iv, s2))
                    link(v.tensor_tensor(a, a2, wide(iv, n), ALU.mult))
                    v.scalar_tensor_tensor(gates[:, g % 2, 0:n, :], a, THRESH, a, ALU.is_gt, ALU.mult)\
                        .then_inc(gates_ready, 1)

            def gated(st):
                _, g, e = st
                if e == 0:
                    dve.wait_ge(gates_ready, g + 1)
                wait_full(dve, st)
                if e > 0:
                    wait_moved(dve, ("gated", g, e - 1))
                src = shared_bank(st)
                for b in range(SIZES[g]):
                    r = resid[:, START[g] + b, :]
                    ins = v.scalar_tensor_tensor(r, src[:, b * C:(b + 1) * C], gates[:, g % 2, b, e:e + 1], r,
                                                 ALU.mult, ALU.add)
                moved(ins, st)

            run = {"stats": stats, "norm": norm, "turn": turn, "maximum": maximum,
                   "exponent": exponent, "weighted": weighted, "scan_den": scan_den, "scan_num": scan_num,
                   "numerator": numerator, "receive": receive, "inverse": inverse, "rwkv": rwkv_,
                   "threshold": threshold, "mixed": mixed, "query": query, "context": context,
                   "scores": scores, "probs_v": probs_v,
                   "attended": attended, "router": router, "gated": gated}
            for st in program("vector"):
                if st[0] in run:
                    run[st[0]](st)

        @block.tensor
        def _(pe):
            mm = nc.tensor.matmul
            pe.wait_ge(pack_in, 16)
            pe.wait_ge(dve_const, 1)
            pe.wait_ge(pool_const, 1)

            def turn(st):
                _, k, g, b = st
                pe.wait_ge(normed, nth[("norm", k, g, CHUNKS[g] - 1 if b is None else b)])
                wait_bank(pe, st)
                for n, i in enumerate(batches(k, g, b)):
                    src = xn_attend[:, i % 2, :] if k == 2 else xn_mix[:, n, :]
                    ins = nc.tensor.transpose(shared_bank(st)[:, n * T:(n + 1) * T], src, ident)
                fill_done(ins, st)

            def project(st, i):
                g = st[1]
                wait_moved(pe, ("turn", 0, g, None))
                wait_bank(pe, st)
                dst, src = by_batch(shared_bank(st)[:, 0:ctok(g)]), xT1[:, 0:npad(g)]
                mm(dst, w_now[:, i, :], now(src), start=True, stop=False)
                fill_done(mm(dst, w_before[:, i, :], before(src), start=False, stop=True), st)

            def mixed(st):
                g = st[1]
                pe.wait_ge(rwkv_ready, g + 1)
                wait_bank(pe, st)
                for b in range(CHUNKS[g]):
                    ins = mm(shared_bank(st)[:, b * C:(b + 1) * C], ta[:, b * T:(b + 1) * T], part("woT"),
                             start=True, stop=True)
                fill_done(ins, st)

            def query(st):
                wait_moved(pe, ("turn", 1, st[1], None))
                wait_bank(pe, st)
                n = ctok(st[1])
                fill_done(mm(shared_bank(st)[:, 0:n], part("Wq"), xT2[:, 0:n], start=True, stop=True), st)

            def context(st):
                i = nth[st] - 1
                if i == 0:
                    pe.wait_ge(ctx_in, 32)
                pe.wait_ge(ctx4_ready, i + 1)
                wait_bank(pe, st)
                dst = shared_bank(st)
                mm(dst[:, 0:M], w96[:, 0:C], ctx_sb[:, i, :], start=True, stop=True)
                for k in range(KT):
                    ins = mm(dst[:, P + k * C:P + (k + 1) * C], ctx4[:, i % CTX_RING, k * P:(k + 1) * P],
                             w96[:, C:2 * C], start=True, stop=True)
                fill_done(ins, st)

            def scores(st):
                _, g, u = st
                n = nth[st] - 1
                i, q = n // NQ, u % NQ
                c, place = chunk_of(i)
                if place == 0 and q == 0:
                    pe.wait_ge(q_in, QUERIES_IN * (c + 1))
                if q == 0:
                    wait_stacked(pe, i)
                if n == 0:
                    pe.wait_ge(ones_ready, 1)
                if n >= 2:
                    pe.wait_ge(scores_read, n - 1)
                mm(bank_s[n % 2][:, 0:SQ], q_stack[:, q, place * T:(place + 1) * T], k_stack[:, i % 2, q, :],
                   start=True, stop=True).then_inc(scores_full, 1)

            def turn_probs(st):
                n = nth[st] - 1
                pe.wait_ge(exp_ready, n + 1)
                if n >= 1:
                    pe.wait_ge(probT_ready, n)
                for k in range(KT):
                    ins = nc.tensor.transpose(bank_p[:, k * P:(k + 1) * P], prob[:, n % PROBS, k * P:(k + 1) * P],
                                              ident)
                ins.then_inc(probs_turned, 1)

            def probs_v(st):
                _, g, u = st
                n = nth[st] - 1
                i, q = n // NQ, n % NQ
                pe.wait_ge(probT_ready, n + 1)
                if q == 0:
                    wait_moved(pe, ("context", g, u // NQ))
                wait_bank(pe, st)
                w = QH * (HD + 1)
                for k in range(KT):
                    at = (k * H + q * QH) * (HD + 1)
                    ins = mm(shared_bank(st)[:, 0:w], probT[:, n % 3, k * P:(k + 1) * P],
                             vbd[:, i % 3, at:at + w], start=(k == 0), stop=(k == KT - 1))
                fill_done(ins, st)

            def turn_heads(st):
                _, g, b = st
                i = nth[st] - 1
                wait_moved(pe, ("probs_v", g, NQ * b + NQ - 1))
                wait_moved(pe, ("probs_v", g, NQ * b + NQ - 2))
                wait_bank(pe, st)
                fill_done(nc.tensor.transpose(shared_bank(st)[:, 0:T], heads[:, i % 2, :], ident), st)

            def attended(st):
                i = nth[st] - 1
                wait_moved(pe, ("turn_heads", st[1], st[2]))
                wait_bank(pe, st)
                fill_done(mm(shared_bank(st)[:, 0:C], headsT[:, i % 2, :], part("Wo"), start=True, stop=True), st)

            def router(st):
                g = st[1]
                for b in range(SIZES[g]):
                    wait_moved(pe, ("turn", 2, g, b))
                wait_bank(pe, st)
                for b in range(SIZES[g]):
                    dst = shared_bank(st)[:, b * E:(b + 1) * E]
                    mm(dst, xT3[:, b * T:(b + 1) * T], part("Wr"), start=True, stop=False)
                    ins = mm(dst, ones_f[0:1, :], br_sb[0:1, :], start=False, stop=True)
                fill_done(ins, st)

            def hidden(st):
                _, g, s = st
                n = nth[st] - 1
                if s == 0:
                    pe.wait_ge(hi_ready, START[g] + SIZES[g])
                    pe.wait_ge(lo_ready, START[g] + SIZES[g])
                if g == 0 and s % FT == 0:
                    pe.wait_ge(w_split, 2 * (s // FT) + 1)
                if n >= 2:
                    pe.wait_ge(hid_ready, n - 1)
                at = slice(s * P, (s + 1) * P)
                z, hi, lo = bank_z[n % 2][:, 0:tok(g)], x_hi[:, g % 2, 0:tok(g)], x_lo[:, g % 2, 0:tok(g)]
                mm(z, w1_lo[:, at], hi, start=True, stop=False)
                mm(z, w1_hi[:, at], lo, start=False, stop=False)
                mm(z, w1_hi[:, at], hi, start=False, stop=True).then_inc(z_full, 1)

            def down(st):
                _, g, s = st
                n = nth[st] - 1
                if g == 0 and s % FT == 0:
                    pe.wait_ge(w_split, 2 * (s // FT) + 2)
                pe.wait_ge(hid_split, n + 1)
                if s % FT == 0 and n > 0:
                    pe.wait_ge(y_ready, n // FT)
                at = slice(s * C, (s + 1) * C)
                y, hi, lo = bank_y[:, 0:tok(g)], hid_hi[:, n % HIDS, 0:tok(g)], hid_lo[:, n % HIDS, 0:tok(g)]
                mm(y, w2_lo[:, at], hi, start=(s % FT == 0), stop=False)
                mm(y, w2_hi[:, at], hi, start=False, stop=False)
                ins = mm(y, w2_hi[:, at], lo, start=False, stop=(s % FT == FT - 1))
                if s % FT == FT - 1:
                    ins.then_inc(y_full, 1)
                else:
                    ins.then_inc(hid_used, 1)

            def gated(st):
                n = nth[st] - 1
                pe.wait_ge(y_ready, n + 1)
                wait_bank(pe, st)
                for b in range(SIZES[st[1]]):
                    ins = nc.tensor.transpose(shared_bank(st)[:, b * C:(b + 1) * C],
                                              yT[:, n % 2, b * T:(b + 1) * T], ident)
                fill_done(ins, st)

            run = {"turn": turn, "key": lambda st: project(st, 0), "value": lambda st: project(st, 1),
                   "receptance": lambda st: project(st, 2), "mixed": mixed, "query": query,
                   "context": context, "scores": scores, "turn_probs": turn_probs, "probs_v": probs_v,
                   "turn_heads": turn_heads, "attended": attended, "router": router, "hidden": hidden,
                   "down": down, "gated": gated}
            for st in program("tensor"):
                if st[0] in run:
                    run[st[0]](st)


def kernel(x, ctx_768, mask_BxS2_bf1, L0_attn_wk, L0_attn_wv, L0_attn_wr, L0_attn_wo, L0_attn_time_decay,
           L0_attn_time_first, L0_attn_mix_k, L0_attn_mix_v, L0_attn_mix_r, L0_xattn_Wq, L0_xattn_Wk,
           L0_xattn_Wv, L0_xattn_Wo, L0_ffn_Wr, L0_ffn_br, L0_ffn_W1, L0_ffn_b1, L0_ffn_W2, L0_ffn_b2):
    import numpy as np
    import concourse.bacc as bacc
    from concourse.bass_utils import run_bass_kernel_spmd

    f32 = np.float32
    ident = np.eye(P, dtype=f32)
    c, h = np.arange(P)[:, None], np.arange(QH)[None, :]
    qmask = ((c // HD) % QH == h).astype(f32) * f32(HD ** -0.5)
    r = np.arange(KT * P).reshape(KT, P).T[:, :, None]
    vmask = (r // M == np.arange(H)[None, None, :] % QH).astype(f32).reshape(P, KT * H)
    cols = np.stack([np.asarray(a).reshape(C) for a in
                     (L0_attn_time_decay, L0_attn_time_first, L0_attn_mix_k, L0_attn_mix_v, L0_attn_mix_r)], 1)
    b1 = np.asarray(L0_ffn_b1).reshape(NS, P).T
    pack = np.concatenate([ident, qmask, vmask, cols, np.asarray(L0_attn_wk).T, np.asarray(L0_attn_wv).T,
                           np.asarray(L0_attn_wr).T, np.asarray(L0_attn_wo).T, np.asarray(L0_xattn_Wq),
                           np.asarray(L0_xattn_Wo), np.asarray(L0_ffn_Wr), b1, np.asarray(L0_ffn_b2).T], 1)
    arrays = {
        "x": np.asarray(x).transpose(1, 0, 2),
        "ctxT": np.asarray(ctx_768).transpose(2, 0, 1),
        "mask": np.asarray(mask_BxS2_bf1).reshape(1, B * M).view(np.uint8),
        "pack": pack,
        "wkv96": np.concatenate([np.asarray(L0_xattn_Wk), np.asarray(L0_xattn_Wv)], 1),
        "br": np.asarray(L0_ffn_br).reshape(1, E),
        "w1": np.asarray(L0_ffn_W1).transpose(1, 0, 2).reshape(P, E * F),
        "w2": np.asarray(L0_ffn_W2).reshape(NS, P, C).transpose(1, 0, 2).reshape(P, NS * C),
    }
    arrays = {n: np.ascontiguousarray(a) for n, a in arrays.items()}
    nc = bacc.Bacc("TRN2", target_bir_lowering=False, num_devices=1)
    args = [nc.dram_tensor(n, a.shape, mybir.dt.from_np(a.dtype), kind="ExternalInput").ap()
            for n, a in arrays.items()]
    args.append(nc.dram_tensor("out", (T, B, C), F32, kind="ExternalOutput").ap())
    build(nc, *args)
    got = run_bass_kernel_spmd(nc, [arrays], core_ids=[0]).results[0]["out"]
    return np.ascontiguousarray(got.transpose(1, 0, 2))
```
